# Optimizing a Trainium2 kernel written in Bass

```python
import numpy as np
import jax
import jax.numpy as jnp

def _softmax(x, axis=-1):
    return jax.nn.softmax(x, axis=axis)

def _gelu(x):
    return jax.nn.gelu(x, approximate=True)

def _silu(x):
    return jax.nn.silu(x)

def _sigmoid(x):
    return jax.nn.sigmoid(x)

def _layernorm(x, axis=-1, eps=1e-05):
    m = jnp.mean(x, axis=axis, keepdims=True)
    v = jnp.var(x, axis=axis, keepdims=True)
    return (x - m) / jnp.sqrt(v + eps)

def _scatter_add(tgt, idx, src, axis=0):
    return tgt.at[idx].add(src)

def _segment_sum(src, seg, n):
    return jax.ops.segment_sum(src, seg, n)
kernel_name = 'mk_hybrid_d1_jaxref_r8_57f6af'

def setup_inputs(seed: int=0):
    np.random.seed(seed)
    _w = jnp.asarray

    def _L0_attn_a_setup():
        import jax, jax.numpy as jnp
        import numpy as np
        B, T, C, FFN, N_LAYER, LAYER_ID = (4, 256, 128, 512, 24, 1)
        EPS = 1e-05

        def _ln(z, g, b):
            m = jnp.mean(z, axis=-1, keepdims=True)
            v = jnp.mean(jnp.square(z - m), axis=-1, keepdims=True)
            return (z - m) * jax.lax.rsqrt(v + EPS) * g + b

        def _shift(z):
            return jnp.pad(z, ((0, 0), (1, 0), (0, 0)))[:, :-1]

        def _wkv(time_decay, u, k, v):
            w = -jnp.exp(time_decay)
            kt = jnp.moveaxis(k, 1, 0)
            vt = jnp.moveaxis(v, 1, 0)
            aa = jnp.zeros_like(kt[0])
            bb = jnp.zeros_like(kt[0])
            pp = jnp.full_like(kt[0], -1e+38)

            def step(carry, kv):
                aa, bb, pp = carry
                kk, vv = kv
                ww = u + kk
                p = jnp.maximum(pp, ww)
                e1 = jnp.exp(pp - p)
                e2 = jnp.exp(ww - p)
                out = (e1 * aa + e2 * vv) / (e1 * bb + e2)
                ww2 = pp + w
                p2 = jnp.maximum(ww2, kk)
                e1b = jnp.exp(ww2 - p2)
                e2b = jnp.exp(kk - p2)
                return ((e1b * aa + e2b * vv, e1b * bb + e2b, p2), out)
            _, out = jax.lax.scan(step, (aa, bb, pp), (kt, vt))
            return jnp.moveaxis(out, 0, 1)
        key = jax.random.key(seed)
        ks = jax.random.split(key, 10)
        scale = 0.02

        def w(k, shape):
            return jax.random.normal(k, shape, jnp.float32) * scale
        r01 = LAYER_ID / (N_LAYER - 1)
        r10 = 1.0 - LAYER_ID / N_LAYER
        ddd = np.arange(C, dtype=np.float64) / C
        h = np.arange(C, dtype=np.float64)
        decay = -5.0 + 8.0 * (h / (C - 1)) ** (0.7 + 1.3 * r01)
        zigzag = np.array([(i + 1) % 3 - 1 for i in range(C)], dtype=np.float64) * 0.5
        tfirst = np.log(0.3) + zigzag
        return {'x': jax.random.normal(ks[0], (B, T, C), jnp.float32), 'ln1_w': jnp.ones((C,), jnp.float32), 'ln1_b': jnp.zeros((C,), jnp.float32), 'ln2_w': jnp.ones((C,), jnp.float32), 'ln2_b': jnp.zeros((C,), jnp.float32), 'time_decay': jnp.asarray(decay, jnp.float32), 'time_first': jnp.asarray(tfirst, jnp.float32), 'tmk': jnp.asarray(ddd ** r10, jnp.float32), 'tmv': jnp.asarray(ddd ** r10 + 0.3 * r01, jnp.float32), 'tmr': jnp.asarray(ddd ** (0.5 * r10), jnp.float32), 'att_kw': w(ks[1], (C, C)), 'att_vw': w(ks[2], (C, C)), 'att_rw': w(ks[3], (C, C)), 'att_ow': w(ks[4], (C, C)), 'f_tmk': jnp.asarray(ddd ** r10, jnp.float32), 'f_tmr': jnp.asarray(ddd ** r10, jnp.float32), 'f_kw': w(ks[5], (FFN, C)), 'f_rw': w(ks[6], (C, C)), 'f_vw': w(ks[7], (C, FFN))}
    _L0_attn_a_in = _L0_attn_a_setup()

    def _L0_attn_b_setup():
        import jax, jax.numpy as jnp
        from jax import lax
        import numpy as np
        import math
        D_MODEL = 128
        D_STATE = 16
        D_CONV = 4
        EXPAND = 2
        D_INNER = EXPAND * D_MODEL
        DT_RANK = math.ceil(D_MODEL / 16)
        BATCH = 2
        SEQ = 256

        def _layernorm(x, w, b):
            mu = x.mean(-1, keepdims=True)
            var = ((x - mu) ** 2).mean(-1, keepdims=True)
            return (x - mu) * lax.rsqrt(var + 1e-05) * w + b

        def _mamba(xn, in_proj_w, conv_w, conv_b, x_proj_w, dt_proj_w, dt_proj_b, A_log, D_skip, out_proj_w):
            xz = xn @ in_proj_w
            xi, z = jnp.split(xz, 2, axis=-1)
            xc = jnp.pad(xi.transpose(0, 2, 1), ((0, 0), (0, 0), (D_CONV - 1, 0)))
            xc = lax.conv_general_dilated(xc, conv_w[:, None, :], (1,), 'VALID', feature_group_count=D_INNER, dimension_numbers=('NCH', 'OIH', 'NCH'))
            xc = jax.nn.silu(xc.transpose(0, 2, 1) + conv_b)
            dbc = xc @ x_proj_w
            dt = jax.nn.softplus(dbc[..., :DT_RANK] @ dt_proj_w + dt_proj_b)
            Bm = dbc[..., DT_RANK:DT_RANK + D_STATE]
            Cm = dbc[..., DT_RANK + D_STATE:]
            A = -jnp.exp(A_log)

            def step(h, inp):
                u_t, dt_t, b_t, c_t = inp
                h = jnp.exp(dt_t[..., None] * A) * h + (dt_t * u_t)[..., None] * b_t[:, None, :]
                y = jnp.einsum('bds,bs->bd', h, c_t)
                return (h, y)
            h0 = jnp.zeros((xn.shape[0], D_INNER, D_STATE), xn.dtype)
            _, ys = lax.scan(step, h0, (xc.transpose(1, 0, 2), dt.transpose(1, 0, 2), Bm.transpose(1, 0, 2), Cm.transpose(1, 0, 2)))
            y = ys.transpose(1, 0, 2) + xc * D_skip
            y = y * jax.nn.silu(z)
            return y @ out_proj_w
        key = jax.random.key(seed)
        ks = jax.random.split(key, 8)
        s = 0.02
        x = jax.random.normal(ks[0], (BATCH, SEQ, D_MODEL), jnp.float32)
        ln_w = jnp.ones((D_MODEL,), jnp.float32)
        ln_b = jnp.zeros((D_MODEL,), jnp.float32)
        in_proj_w = jax.random.normal(ks[1], (D_MODEL, 2 * D_INNER), jnp.float32) * s
        conv_w = jax.random.normal(ks[2], (D_INNER, D_CONV), jnp.float32) * s
        conv_b = jnp.zeros((D_INNER,), jnp.float32)
        x_proj_w = jax.random.normal(ks[3], (D_INNER, DT_RANK + 2 * D_STATE), jnp.float32) * s
        dt_proj_w = jax.random.normal(ks[4], (DT_RANK, D_INNER), jnp.float32) * DT_RANK ** (-0.5)
        dt = jnp.exp(jax.random.uniform(ks[5], (D_INNER,), jnp.float32) * (jnp.log(0.1) - jnp.log(0.001)) + jnp.log(0.001))
        dt_proj_b = dt + jnp.log(-jnp.expm1(-dt))
        A_log = jnp.log(jnp.broadcast_to(jnp.arange(1, D_STATE + 1, dtype=jnp.float32), (D_INNER, D_STATE)))
        D_skip = jnp.ones((D_INNER,), jnp.float32)
        out_proj_w = jax.random.normal(ks[6], (D_INNER, D_MODEL), jnp.float32) * s
        return dict(x=x, ln_w=ln_w, ln_b=ln_b, in_proj_w=in_proj_w, conv_w=conv_w, conv_b=conv_b, x_proj_w=x_proj_w, dt_proj_w=dt_proj_w, dt_proj_b=dt_proj_b, A_log=A_log, D_skip=D_skip, out_proj_w=out_proj_w)
    _L0_attn_b_in = _L0_attn_b_setup()

    def _L0_ffn_setup():
        import jax, jax.numpy as jnp
        import numpy as np
        DIM = 128
        HIDDEN = 384
        SCALE = 1.0 / 127.0

        def _dequant(w_int, dtype):
            return w_int.astype(dtype) * jnp.asarray(SCALE, dtype)
        key = jax.random.key(seed)
        k_x, k_g, k_u, k_d = jax.random.split(key, 4)
        x = jax.random.normal(k_x, (4, 256, DIM), dtype=jnp.float32)
        w_gate = jax.random.randint(k_g, (HIDDEN, DIM), -127, 128, dtype=jnp.int32)
        w_up = jax.random.randint(k_u, (HIDDEN, DIM), -127, 128, dtype=jnp.int32)
        w_down = jax.random.randint(k_d, (DIM, HIDDEN), -127, 128, dtype=jnp.int32)
        return {'x': x, 'w_gate': w_gate, 'w_up': w_up, 'w_down': w_down}
    _L0_ffn_in = _L0_ffn_setup()
    _d = {'L0_attn_a_x': _L0_attn_a_in['x'], 'L0_attn_a_ln1_w': _L0_attn_a_in['ln1_w'], 'L0_attn_a_ln1_b': _L0_attn_a_in['ln1_b'], 'L0_attn_a_ln2_w': _L0_attn_a_in['ln2_w'], 'L0_attn_a_ln2_b': _L0_attn_a_in['ln2_b'], 'L0_attn_a_time_decay': _L0_attn_a_in['time_decay'], 'L0_attn_a_time_first': _L0_attn_a_in['time_first'], 'L0_attn_a_tmk': _L0_attn_a_in['tmk'], 'L0_attn_a_tmv': _L0_attn_a_in['tmv'], 'L0_attn_a_tmr': _L0_attn_a_in['tmr'], 'L0_attn_a_att_kw': _L0_attn_a_in['att_kw'], 'L0_attn_a_att_vw': _L0_attn_a_in['att_vw'], 'L0_attn_a_att_rw': _L0_attn_a_in['att_rw'], 'L0_attn_a_att_ow': _L0_attn_a_in['att_ow'], 'L0_attn_a_f_tmk': _L0_attn_a_in['f_tmk'], 'L0_attn_a_f_tmr': _L0_attn_a_in['f_tmr'], 'L0_attn_a_f_kw': _L0_attn_a_in['f_kw'], 'L0_attn_a_f_rw': _L0_attn_a_in['f_rw'], 'L0_attn_a_f_vw': _L0_attn_a_in['f_vw'], 'L0_attn_b_ln_w': _L0_attn_b_in['ln_w'], 'L0_attn_b_ln_b': _L0_attn_b_in['ln_b'], 'L0_attn_b_in_proj_w': _L0_attn_b_in['in_proj_w'], 'L0_attn_b_conv_w': _L0_attn_b_in['conv_w'], 'L0_attn_b_conv_b': _L0_attn_b_in['conv_b'], 'L0_attn_b_x_proj_w': _L0_attn_b_in['x_proj_w'], 'L0_attn_b_dt_proj_w': _L0_attn_b_in['dt_proj_w'], 'L0_attn_b_dt_proj_b': _L0_attn_b_in['dt_proj_b'], 'L0_attn_b_A_log': _L0_attn_b_in['A_log'], 'L0_attn_b_D_skip': _L0_attn_b_in['D_skip'], 'L0_attn_b_out_proj_w': _L0_attn_b_in['out_proj_w'], 'L0_ffn_w_gate': _L0_ffn_in['w_gate'], 'L0_ffn_w_up': _L0_ffn_in['w_up'], 'L0_ffn_w_down': _L0_ffn_in['w_down']}
    _x0 = _d['L0_attn_a_x']
    _d['L0_attn_a_x'] = jax.random.normal(jax.random.fold_in(jax.random.key(seed), 1), (4, 512, 128), dtype=_x0.dtype)
    del _x0
    return _d

def reference(L0_attn_a_x, L0_attn_a_ln1_w, L0_attn_a_ln1_b, L0_attn_a_ln2_w, L0_attn_a_ln2_b, L0_attn_a_time_decay, L0_attn_a_time_first, L0_attn_a_tmk, L0_attn_a_tmv, L0_attn_a_tmr, L0_attn_a_att_kw, L0_attn_a_att_vw, L0_attn_a_att_rw, L0_attn_a_att_ow, L0_attn_a_f_tmk, L0_attn_a_f_tmr, L0_attn_a_f_kw, L0_attn_a_f_rw, L0_attn_a_f_vw, L0_attn_b_ln_w, L0_attn_b_ln_b, L0_attn_b_in_proj_w, L0_attn_b_conv_w, L0_attn_b_conv_b, L0_attn_b_x_proj_w, L0_attn_b_dt_proj_w, L0_attn_b_dt_proj_b, L0_attn_b_A_log, L0_attn_b_D_skip, L0_attn_b_out_proj_w, L0_ffn_w_gate, L0_ffn_w_up, L0_ffn_w_down):

    def _L0_attn_a_ref(x, ln1_w, ln1_b, ln2_w, ln2_b, time_decay, time_first, tmk, tmv, tmr, att_kw, att_vw, att_rw, att_ow, f_tmk, f_tmr, f_kw, f_rw, f_vw):
        import jax, jax.numpy as jnp
        import numpy as np
        B, T, C, FFN, N_LAYER, LAYER_ID = (4, 256, 128, 512, 24, 1)
        EPS = 1e-05

        def _ln(z, g, b):
            m = jnp.mean(z, axis=-1, keepdims=True)
            v = jnp.mean(jnp.square(z - m), axis=-1, keepdims=True)
            return (z - m) * jax.lax.rsqrt(v + EPS) * g + b

        def _shift(z):
            return jnp.pad(z, ((0, 0), (1, 0), (0, 0)))[:, :-1]

        def _wkv(time_decay, u, k, v):
            w = -jnp.exp(time_decay)
            kt = jnp.moveaxis(k, 1, 0)
            vt = jnp.moveaxis(v, 1, 0)
            aa = jnp.zeros_like(kt[0])
            bb = jnp.zeros_like(kt[0])
            pp = jnp.full_like(kt[0], -1e+38)

            def step(carry, kv):
                aa, bb, pp = carry
                kk, vv = kv
                ww = u + kk
                p = jnp.maximum(pp, ww)
                e1 = jnp.exp(pp - p)
                e2 = jnp.exp(ww - p)
                out = (e1 * aa + e2 * vv) / (e1 * bb + e2)
                ww2 = pp + w
                p2 = jnp.maximum(ww2, kk)
                e1b = jnp.exp(ww2 - p2)
                e2b = jnp.exp(kk - p2)
                return ((e1b * aa + e2b * vv, e1b * bb + e2b, p2), out)
            _, out = jax.lax.scan(step, (aa, bb, pp), (kt, vt))
            return jnp.moveaxis(out, 0, 1)
        h = _ln(x, ln1_w, ln1_b)
        hx = _shift(h)
        xk = h * tmk + hx * (1.0 - tmk)
        xv = h * tmv + hx * (1.0 - tmv)
        xr = h * tmr + hx * (1.0 - tmr)
        k = jnp.einsum('btc,dc->btd', xk, att_kw)
        v = jnp.einsum('btc,dc->btd', xv, att_vw)
        sr = jax.nn.sigmoid(jnp.einsum('btc,dc->btd', xr, att_rw))
        rwkv = sr * _wkv(time_decay, time_first, k, v)
        x = x + jnp.einsum('btd,cd->btc', rwkv, att_ow)
        h = _ln(x, ln2_w, ln2_b)
        hx = _shift(h)
        xk = h * f_tmk + hx * (1.0 - f_tmk)
        xr = h * f_tmr + hx * (1.0 - f_tmr)
        kk = jnp.square(jax.nn.relu(jnp.einsum('btc,fc->btf', xk, f_kw)))
        kv = jnp.einsum('btf,cf->btc', kk, f_vw)
        x = x + jax.nn.sigmoid(jnp.einsum('btc,dc->btd', xr, f_rw)) * kv
        return x

    def _L0_attn_b_ref(x, ln_w, ln_b, in_proj_w, conv_w, conv_b, x_proj_w, dt_proj_w, dt_proj_b, A_log, D_skip, out_proj_w):
        import jax, jax.numpy as jnp
        from jax import lax
        import numpy as np
        import math
        D_MODEL = 128
        D_STATE = 16
        D_CONV = 4
        EXPAND = 2
        D_INNER = EXPAND * D_MODEL
        DT_RANK = math.ceil(D_MODEL / 16)
        BATCH = 2
        SEQ = 256

        def _layernorm(x, w, b):
            mu = x.mean(-1, keepdims=True)
            var = ((x - mu) ** 2).mean(-1, keepdims=True)
            return (x - mu) * lax.rsqrt(var + 1e-05) * w + b

        def _mamba(xn, in_proj_w, conv_w, conv_b, x_proj_w, dt_proj_w, dt_proj_b, A_log, D_skip, out_proj_w):
            xz = xn @ in_proj_w
            xi, z = jnp.split(xz, 2, axis=-1)
            xc = jnp.pad(xi.transpose(0, 2, 1), ((0, 0), (0, 0), (D_CONV - 1, 0)))
            xc = lax.conv_general_dilated(xc, conv_w[:, None, :], (1,), 'VALID', feature_group_count=D_INNER, dimension_numbers=('NCH', 'OIH', 'NCH'))
            xc = jax.nn.silu(xc.transpose(0, 2, 1) + conv_b)
            dbc = xc @ x_proj_w
            dt = jax.nn.softplus(dbc[..., :DT_RANK] @ dt_proj_w + dt_proj_b)
            Bm = dbc[..., DT_RANK:DT_RANK + D_STATE]
            Cm = dbc[..., DT_RANK + D_STATE:]
            A = -jnp.exp(A_log)

            def step(h, inp):
                u_t, dt_t, b_t, c_t = inp
                h = jnp.exp(dt_t[..., None] * A) * h + (dt_t * u_t)[..., None] * b_t[:, None, :]
                y = jnp.einsum('bds,bs->bd', h, c_t)
                return (h, y)
            h0 = jnp.zeros((xn.shape[0], D_INNER, D_STATE), xn.dtype)
            _, ys = lax.scan(step, h0, (xc.transpose(1, 0, 2), dt.transpose(1, 0, 2), Bm.transpose(1, 0, 2), Cm.transpose(1, 0, 2)))
            y = ys.transpose(1, 0, 2) + xc * D_skip
            y = y * jax.nn.silu(z)
            return y @ out_proj_w
        xn = _layernorm(x, ln_w, ln_b)
        return x + _mamba(xn, in_proj_w, conv_w, conv_b, x_proj_w, dt_proj_w, dt_proj_b, A_log, D_skip, out_proj_w)

    def _L0_ffn_ref(x, w_gate, w_up, w_down):
        import jax, jax.numpy as jnp
        import numpy as np
        DIM = 128
        HIDDEN = 384
        SCALE = 1.0 / 127.0

        def _dequant(w_int, dtype):
            return w_int.astype(dtype) * jnp.asarray(SCALE, dtype)
        wg = _dequant(w_gate, x.dtype)
        wu = _dequant(w_up, x.dtype)
        wd = _dequant(w_down, x.dtype)
        gate = jnp.einsum('bsd,hd->bsh', x, wg)
        up = jnp.einsum('bsd,hd->bsh', x, wu)
        h = jax.nn.silu(gate) * up
        return jnp.einsum('bsh,dh->bsd', h, wd)
    x = L0_attn_a_x
    x = x + _L0_attn_a_ref(_layernorm(x, axis=-1), L0_attn_a_ln1_w, L0_attn_a_ln1_b, L0_attn_a_ln2_w, L0_attn_a_ln2_b, L0_attn_a_time_decay, L0_attn_a_time_first, L0_attn_a_tmk, L0_attn_a_tmv, L0_attn_a_tmr, L0_attn_a_att_kw, L0_attn_a_att_vw, L0_attn_a_att_rw, L0_attn_a_att_ow, L0_attn_a_f_tmk, L0_attn_a_f_tmr, L0_attn_a_f_kw, L0_attn_a_f_rw, L0_attn_a_f_vw)
    x = x + _L0_ffn_ref(_layernorm(x, axis=-1), L0_ffn_w_gate, L0_ffn_w_up, L0_ffn_w_down)
    x = x + _L0_attn_b_ref(_layernorm(x, axis=-1), L0_attn_b_ln_w, L0_attn_b_ln_b, L0_attn_b_in_proj_w, L0_attn_b_conv_w, L0_attn_b_conv_b, L0_attn_b_x_proj_w, L0_attn_b_dt_proj_w, L0_attn_b_dt_proj_b, L0_attn_b_A_log, L0_attn_b_D_skip, L0_attn_b_out_proj_w)
    x = x + _L0_ffn_ref(_layernorm(x, axis=-1), L0_ffn_w_gate, L0_ffn_w_up, L0_ffn_w_down)
    return x

_drawn_inputs = setup_inputs


def setup_inputs(seed=0):
    import zlib

    import numpy as np

    out = dict(_drawn_inputs(seed))
    spreads = {'L0_attn_a_ln1_w': (1.0, 0.6),
     'L0_attn_a_ln1_b': (0.0, 0.8),
     'L0_attn_a_ln2_w': (1.0, 0.6),
     'L0_attn_a_ln2_b': (0.0, 0.8),
     'L0_attn_b_ln_w': (1.0, 0.6),
     'L0_attn_b_ln_b': (0.0, 0.8),
     'L0_attn_b_conv_b': (0.0, 0.8),
     'L0_attn_b_D_skip': (1.0, 0.6)}
    factors = {'L0_attn_a_time_decay': 6.737,
     'L0_attn_a_time_first': 8.0,
     'L0_attn_a_tmk': 8.0,
     'L0_attn_a_tmv': 8.0,
     'L0_attn_a_tmr': 8.0,
     'L0_attn_a_att_kw': 8.0,
     'L0_attn_a_att_vw': 4.567,
     'L0_attn_a_att_rw': 8.0,
     'L0_attn_a_att_ow': 4.528,
     'L0_attn_a_f_tmk': 8.0,
     'L0_attn_a_f_tmr': 8.0,
     'L0_attn_a_f_kw': 6.522,
     'L0_attn_a_f_rw': 8.0,
     'L0_attn_a_f_vw': 6.082,
     'L0_attn_b_in_proj_w': 8.0,
     'L0_attn_b_conv_w': 8.0,
     'L0_attn_b_x_proj_w': 8.0,
     'L0_attn_b_dt_proj_w': 8.0,
     'L0_attn_b_dt_proj_b': 8.0,
     'L0_attn_b_A_log': 8.0,
     'L0_attn_b_out_proj_w': 8.0}
    for name, (base, spread) in spreads.items():
        noise = np.random.default_rng([zlib.crc32(name.encode()), seed]).standard_normal(out[name].shape)
        drawn = base * np.exp(spread * noise) if base else spread * noise
        out[name] = jnp.asarray(drawn.astype(out[name].dtype))
    for name, factor in factors.items():
        out[name] = (out[name] * factor).astype(out[name].dtype)
    return out
```

```python
from contextlib import ExitStack

import concourse.bass as bass
from concourse import mybir

ALU = mybir.AluOpType
ACT = mybir.ActivationFunctionType
F32 = mybir.dt.float32
BF16 = mybir.dt.bfloat16
I32 = mybir.dt.int32

P = 128
B, T, C = 4, 512, 128
NP = 2
RF = 512
RJ = RF // P
HID = 384
HJ = HID // P
DI = 256
DH = DI // P
RANK, NS, TAPS = 8, 16, 4
EPS = 1e-5
WSCALE = 1.0 / 127.0
NB = 2 * T // P

LN1G, LN1B, LN2G, LN2B, DECAY, FIRST, TMK, TMV, TMR, FTMK, FTMR, LNG, LNB = range(13)
CONVW = 13
CONVB = CONVW + DH * TAPS
DTB = CONVB + DH
SKIP = DTB + DH
ALOG = SKIP + DH
NVEC = ALOG + DH * NS


def build(nc, x_in, vec_in, att_in, fkw_in, frw_in, fvw_in, ffn_in, inp_in, xpj_in, dtw_in, outp_in,
          mat_in, sel_in, out):
    with ExitStack() as ctx:
        def sb(name, shape, dt=F32):
            return ctx.enter_context(nc.sbuf_tensor(name, shape, dt))

        def sem(name):
            return ctx.enter_context(nc.semaphore(name))

        def sems(name):
            return [sem(f"{name}{q}") for q in range(NP)]

        vec = sb("vec", [P, NVEC])
        att = sb("att", [P, 4, C])
        fkw = sb("fkw", [P, RF])
        frw = sb("frw", [P, C])
        fvw = sb("fvw", [P, RJ, C])
        ffn = sb("ffn", [P, 3, HID])
        ffn_int = sb("ffn_int", [P, 3, HID], I32)
        inp = sb("inp", [P, 2 * DI])
        xpj = sb("xpj", [P, DH, P])
        dtw = sb("dtw", [RANK, DI])
        outp = sb("outp", [P, DH, C])
        mat = sb("mat", [P, P])
        sel = sb("sel", [P, 2 * NS, P], BF16)
        negw = sb("negw", [P, 1])
        nega = sb("nega", [P, DH * NS])
        ident = mat[:, :]
        stats = [sb(f"stats{q}", [P, NB, 6]) for q in range(NP)]
        moments = [sb(f"moments{q}", [P, NB, 2]) for q in range(NP)]
        rstd = [sb(f"rstd{q}", [P, 2, NB]) for q in range(NP)]
        power = sb("power", [P, 2, NB])

        X = [sb(f"X{q}", [P, 2, T]) for q in range(NP)]
        U = [sb(f"U{q}", [P, 2, T]) for q in range(NP)]
        H = [sb(f"H{q}", [P, 2, T + 1]) for q in range(NP)]
        PP = [sb(f"PP{q}", [P, 2, T + 1]) for q in range(NP)]
        AB = [[sb(f"AB{q}{h}", [P, 2, T + 3]) for h in range(2)] for q in range(NP)]
        TT = [[sb(f"T{q}{i}", [P, 2, T]) for i in range(8)] for q in range(NP)]
        XC = [sb(f"XC{q}", [P, DH, 2, T]) for q in range(NP)]
        SZ = [sb(f"SZ{q}", [P, DH, 2, T]) for q in range(NP)]
        DT = [sb(f"DT{q}", [P, DH, 2, T]) for q in range(NP)]
        DU = [sb(f"DU{q}", [P, DH, 2, T]) for q in range(NP)]
        ST = [H[q][:, :, 0:T // 2].bitcast(BF16) for q in range(NP)]
        CB = [PP[q][:, :, 0:T] for q in range(NP)]
        LOW = [U[q][0:RANK] for q in range(NP)]

        SL = [ctx.enter_context(nc.psum_tensor(f"SL{i}", [P, 2, T], F32)) for i in range(4)]
        PA, PB = [SL[0], SL[2]], [SL[1], SL[3]]
        bank_b, bank_c, bank_y = SL[2][:, 0, :], SL[2][:, 1, :], SL[3]

        loaded_v, loaded_m, loaded_a = sem("loaded_v"), sem("loaded_m"), sem("loaded_a")
        loaded_f, loaded_q, loaded_s, loaded_i = sem("loaded_f"), sem("loaded_q"), sem("loaded_s"), sem("loaded_i")
        x_loaded, out_stored = sems("x_loaded"), sems("out_stored")
        power_set, pads_set, decay_exp, decay_set = sem("power_set"), sem("pads_set"), sem("decay_exp"), sem("decay_set")
        a_exp, a_set, dequantised, halved, taps_halved = (sem(n) for n in ("a_exp", "a_set", "dequantised", "halved", "taps_halved"))
        stats_made, moments_made, var_eps, rstd_made = (sems(n) for n in ("stats_made", "moments_made", "var_eps", "rstd_made"))
        normed, turned = sems("normed"), sems("turned")
        h_made, h_diff, mixed = sems("h_made"), sems("h_diff"), sems("mixed")
        kv_copied = sems("kv_copied")
        projected = sems("projected")
        r_tanh, den_inv, r_scaled = sems("r_tanh"), sems("den_inv"), sems("r_scaled")
        max_run, max_diff = sems("max_run"), sems("max_diff")
        out_diff, wkv_exp, summed = sems("out_diff"), sems("wkv_exp"), sems("summed")
        wkv_step = sems("wkv_step")
        x_att, x_plus = sems("x_att"), sems("x_plus")
        relu, key_sq = sems("relu"), sems("key_sq")
        rec_tanh, chan, x_ready, hn_made = sems("rec_tanh"), sems("chan"), sems("x_ready"), sems("hn_made")
        gate_out, up_out, gate_tanh = sems("gate_out"), sems("up_out"), sems("gate_tanh")
        gated, hidden, down_out = sems("gated"), sems("hidden"), sems("down_out")
        xn_made, in_out, xi_copied = sems("xn_made"), sems("in_out"), sems("xi_copied")
        z_tanh, z_silu, c_tanh = sems("z_tanh"), sems("z_silu"), sems("c_tanh")
        conv, xc_made = sems("conv"), sems("xc_made")
        stacked, rest = sems("stacked"), sems("rest")
        dt_in, dt_exp, dt_log = sems("dt_in"), sems("dt_exp"), sems("dt_log")
        dt_vector = sems("dt_vector")
        dt_pool = sems("dt_pool")
        zeros_set, b_spread, c_spread, c_kept, decayed, driven, scanned, weighed, y_summed, y_taken = (
            sems(n) for n in ("zeros_set", "b_spread", "c_spread", "c_kept", "decayed", "driven", "scanned", "weighed", "y_summed", "y_taken"))
        y_gated, o_out = sems("y_gated"), sems("o_out")

        QS = range(NP)
        x_view = x_in.rearrange("(q n p) c -> q p n c", q=NP, p=P)
        out_view = out.rearrange("(q n p) c -> q p n c", q=NP, p=P)

        def blocks(tile):
            return tile.rearrange("p b (n c) -> p (b n) c", c=P)

        def v(col, n=1):
            return vec[:, col:col + n]

        block = ctx.enter_context(nc.Block())

        @block.sync
        def _(sp):
            sp.dma_start(blocks(X[0]), x_view[0]).then_inc(x_loaded[0], 16)
            sp.dma_start(mat[:], mat_in).then_inc(loaded_m, 16)
            sp.dma_start(blocks(X[1]), x_view[1]).then_inc(x_loaded[1], 16)
            sp.dma_start(vec[:], vec_in).then_inc(loaded_v, 16)
            sp.dma_start(att[:], att_in).then_inc(loaded_a, 16)
            sp.dma_start(fkw[:], fkw_in).then_inc(loaded_f, 16)
            sp.dma_start(frw[:], frw_in).then_inc(loaded_f, 16)
            sp.dma_start(fvw[:], fvw_in).then_inc(loaded_f, 16)
            sp.dma_start(inp[:], inp_in).then_inc(loaded_s, 16)
            sp.dma_start(xpj[:], xpj_in).then_inc(loaded_s, 16)
            sp.dma_start(dtw[:], dtw_in).then_inc(loaded_s, 16)
            sp.dma_start(outp[:], outp_in).then_inc(loaded_s, 16)
            sp.dma_start(sel[:], sel_in).then_inc(loaded_s, 16)
            for q in QS:
                sp.wait_ge(x_ready[q], 4)
                sp.dma_start(out_view[q], blocks(X[q])).then_inc(out_stored[q], 16)
            for q in QS:
                sp.wait_ge(out_stored[q], 16)

        @block.tensor
        def _(pe):
            def product(dst, weights, src, start=True, stop=True):
                for j in range(2):
                    last = nc.tensor.matmul(dst[:, j, :], weights, src[:, j, :], start=start, stop=stop)
                return last

            def turn(k):
                for q in QS:
                    pe.wait_ge(normed[q], k + 1)
                    for n in range(NB):
                        last = nc.tensor.transpose(blocks(PA[q])[:, n, :], blocks(TT[q][0])[:, n, :], ident)
                    last.then_inc(turned[q], 1)

            def back(dst, weights, srcs, n):
                for j, (w, src) in enumerate(zip(weights, srcs)):
                    last = nc.tensor.matmul(blocks(dst)[:, n, :], blocks(src)[:, n, :], w, start=(j == 0),
                                            stop=(j == len(srcs) - 1), skip_group_check=True)
                return last

            pe.wait_ge(loaded_m, 16)
            turn(0)
            pe.wait_ge(loaded_a, 16)
            for q in QS:
                pe.wait_ge(mixed[q], 1)
                product(PA[q], att[:, 0, :], TT[q][4]).then_inc(projected[q], 1)
            for q in QS:
                pe.wait_ge(mixed[q], 2)
                product(PB[q], att[:, 1, :], TT[q][5]).then_inc(projected[q], 1)
            for q in QS:
                pe.wait_ge(mixed[q], 3)
                pe.wait_ge(kv_copied[q], 1)
                product(PA[q], att[:, 2, :], TT[q][6]).then_inc(projected[q], 1)
            for q in QS:
                pe.wait_ge(halved, 2)
                pe.wait_ge(r_scaled[q], 1)
                for n in range(NB):
                    last = back(PB[q], [att[:, 3, :]], [TT[q][3]], n)
                last.then_inc(projected[q], 1)
            turn(1)
            pe.wait_ge(loaded_f, 48)
            for j in range(RJ):
                for q in QS:
                    if j == 0:
                        pe.wait_ge(mixed[q], 4)
                    if j >= 2:
                        pe.wait_ge(relu[q], j - 1)
                    product((PA, PB)[j % 2][q], fkw[:, j * P:(j + 1) * P], TT[q][4]).then_inc(projected[q], 1)
            for q in QS:
                pe.wait_ge(mixed[q], 5)
                pe.wait_ge(relu[q], 3)
                for n in range(NB):
                    last = back(PA[q], [frw[:, :]], [TT[q][5]], n)
                last.then_inc(projected[q], 1)
            for q in QS:
                pe.wait_ge(relu[q], 4)
                pe.wait_ge(key_sq[q], RJ)
                for n in range(NB):
                    last = back(PB[q], [fvw[:, j, :] for j in range(RJ)], [TT[q][j] for j in range(RJ)], n)
                last.then_inc(projected[q], 1)

            def ffn_block(i, k):
                turn(k)
                pe.wait_ge(dequantised, 3)
                for j in range(HJ):
                    n = HJ * i + j
                    for q in QS:
                        if j == 0:
                            pe.wait_ge(hn_made[q], i + 1)
                        else:
                            pe.wait_ge(gated[q], n)
                        product(PA[q], ffn[:, 0, j * P:(j + 1) * P], TT[q][2]).then_inc(gate_out[q], 1)
                    for q in QS:
                        if j > 0:
                            pe.wait_ge(hidden[q], n)
                        product(PB[q], ffn[:, 1, j * P:(j + 1) * P], TT[q][2]).then_inc(up_out[q], 1)
                for q in QS:
                    pe.wait_ge(hidden[q], HJ * (i + 1))
                    for n in range(NB):
                        last = back(PA[q], [ffn[:, 2, j * P:(j + 1) * P] for j in range(HJ)],
                                    [TT[q][4 + j] for j in range(HJ)], n)
                    last.then_inc(down_out[q], 1)

            ffn_block(0, 2)
            turn(3)
            pe.wait_ge(loaded_s, 80)
            for m in range(4):
                for q in QS:
                    if m == 0:
                        pe.wait_ge(xn_made[q], 1)
                    if m == 2:
                        pe.wait_ge(halved, 2)
                    if m >= 2:
                        pe.wait_ge(xi_copied[q], m - 1)
                    product((PA, PB)[m % 2][q], inp[:, m * P:(m + 1) * P], TT[q][4]).then_inc(in_out[q], 1)
            for q in QS:
                pe.wait_ge(z_silu[q], 1)
                for h in range(DH):
                    pe.wait_ge(xc_made[q], h + 1)
                    last = product(PA[q], xpj[:, h, :], XC[q][:, h], start=(h == 0), stop=(h == DH - 1))
                last.then_inc(in_out[q], 1)
            for q in QS:
                pe.wait_ge(stacked[q], 1)
                pe.wait_ge(z_silu[q], 2)
                product(PB[q], dtw[:, 0:P], LOW[q]).then_inc(in_out[q], 1)
            for q in QS:
                pe.wait_ge(rest[q], 1)
                product(PA[q], dtw[:, P:DI], LOW[q]).then_inc(in_out[q], 1)

            def spread(q, j, n, s):
                if not (isinstance(n, int) and n < 1):
                    pe.wait_ge(driven[q], n)
                nc.tensor.matmul(bank_b, sel[:, s, :], ST[q][:, j, :], start=True, stop=True).then_inc(b_spread[q], 1)
                if not (isinstance(n, int) and n < 1):
                    pe.wait_ge(c_kept[q], n)
                nc.tensor.matmul(bank_c, sel[:, NS + s, :], ST[q][:, j, :], start=True, stop=True).then_inc(c_spread[q], 1)

            def total(q, n, ring, start, stop):
                pe.wait_ge(weighed[q], n + 1)
                for h in range(DH):
                    last = nc.tensor.matmul(bank_y[:, h, :], ident, TT[q][6 + ring][:, h, :], start=start, stop=stop,
                                            skip_group_check=True)
                last.then_inc(y_summed[q], 1)

            for q in QS:
                pe.wait_ge(rest[q], 2)
                if q == 0:
                    pe.wait_ge(dt_in[1], 4)
                else:
                    pe.wait_ge(y_taken[0], 4)
                for j in range(2):
                    for s in range(4):
                        n = NS * j + s
                        spread(q, j, n, s)
                        if n >= 2:
                            if n == NS + 2:
                                pe.wait_ge(y_taken[q], 2)
                            total(q, n - 2, s % 2, start=(s == 2), stop=(s == 1))
                    with pe.Fori(2, NS // 2) as i:
                        for r in range(2):
                            spread(q, j, NS * j + 2 * i + r, 2 * i + r)
                            total(q, NS * j + 2 * i + r - 2, r, start=False, stop=False)
                for r in range(2):
                    total(q, 2 * NS - 2 + r, r, start=False, stop=(r == 1))

            for q in QS:
                pe.wait_ge(y_gated[q], DH)
                for n in range(NB):
                    last = back(PA[q], [outp[:, h, :] for h in range(DH)], [XC[q][:, h] for h in range(DH)], n)
                last.then_inc(o_out[q], 1)
            ffn_block(1, 4)

        @block.scalar
        def _(act):
            act.dma_start(ffn_int[:], ffn_in).then_inc(loaded_q, 16)
            act.wait_ge(loaded_v, 16)
            nc.scalar.activation(negw[:], v(DECAY), ACT.Exp).then_inc(decay_exp, 1)
            nc.scalar.activation(nega[:], v(ALOG, DH * NS), ACT.Exp).then_inc(a_exp, 1)
            act.wait_ge(loaded_a, 16)
            nc.scalar.activation(att[:, 3, :], att[:, 3, :], ACT.Copy, scale=0.5).then_inc(halved, 1)
            nc.scalar.activation(v(CONVW, DH * TAPS + DH), v(CONVW, DH * TAPS + DH), ACT.Copy, scale=0.5).then_inc(taps_halved, 1)
            for q in QS:
                act.wait_ge(pads_set, 2)
                act.wait_ge(turned[q], 1)
                nc.scalar.activation(H[q][:, :, 1:T + 1], PA[q][:], ACT.Identity, bias=v(LN1B),
                                     scale=v(LN1G)).then_inc(h_made[q], 1)
            for q in QS:
                act.wait_ge(projected[q], 1)
                nc.scalar.activation(TT[q][0][:], PA[q][:], ACT.Copy).then_inc(kv_copied[q], 1)
            for q in QS:
                act.wait_ge(projected[q], 2)
                nc.scalar.activation(TT[q][1][:], PB[q][:], ACT.Copy).then_inc(kv_copied[q], 1)
            for q in QS:
                act.wait_ge(projected[q], 3)
                nc.scalar.activation(TT[q][2][:], PA[q][:], ACT.Tanh, scale=0.5).then_inc(r_tanh[q], 1)
            act.wait_ge(decay_set, 1)
            for q in QS:
                act.wait_ge(max_diff[q], 1)
                nc.scalar.activation(TT[q][3][:], TT[q][3][:], ACT.Exp, bias=negw[:, 0:1]).then_inc(wkv_exp[q], 1)
                act.wait_ge(max_diff[q], 2)
                nc.scalar.activation(TT[q][4][:], TT[q][4][:], ACT.Exp).then_inc(wkv_exp[q], 1)
            for q in QS:
                act.wait_ge(out_diff[q], 2)
                nc.scalar.activation(TT[q][0][:], TT[q][0][:], ACT.Exp).then_inc(wkv_exp[q], 1)
                act.wait_ge(out_diff[q], 3)
                nc.scalar.activation(TT[q][6][:], TT[q][6][:], ACT.Exp, scale=-1.0).then_inc(wkv_exp[q], 1)
            act.wait_ge(loaded_s, 80)
            nc.scalar.activation(inp[:, DI:2 * DI], inp[:, DI:2 * DI], ACT.Copy, scale=0.5).then_inc(halved, 1)
            for q in QS:
                act.wait_ge(turned[q], 2)
                nc.scalar.activation(H[q][:, :, 1:T + 1], PA[q][:], ACT.Identity, bias=v(LN2B),
                                     scale=v(LN2G)).then_inc(h_made[q], 1)
            for j in range(RJ):
                for q in QS:
                    act.wait_ge(projected[q], 4 + j + 1)
                    if j == 3:
                        act.wait_ge(mixed[q], 5)
                    nc.scalar.activation(TT[q][j][:], (PA, PB)[j % 2][q][:], ACT.Relu).then_inc(relu[q], 1)
            for q in QS:
                act.wait_ge(projected[q], 9)
                nc.scalar.activation(TT[q][6][:], PA[q][:], ACT.Tanh, scale=0.5).then_inc(rec_tanh[q], 1)

            def ffn_block(i, k):
                for q in QS:
                    act.wait_ge(turned[q], k + 1)
                    nc.scalar.activation(TT[q][2][:], PA[q][:], ACT.Copy).then_inc(hn_made[q], 1)
                for j in range(HJ):
                    n = HJ * i + j + 1
                    for q in QS:
                        act.wait_ge(gate_out[q], n)
                        nc.scalar.activation(TT[q][(3, 7)[j % 2]][:], PA[q][:], ACT.Tanh).then_inc(gate_tanh[q], 1)

            act.wait_ge(loaded_q, 16)
            for m in range(3):
                nc.scalar.activation(ffn[:, m, :], ffn_int[:, m, :], ACT.Copy,
                                     scale=WSCALE * 0.5 if m == 0 else WSCALE).then_inc(dequantised, 1)
            ffn_block(0, 2)

            for q in QS:
                act.wait_ge(turned[q], 4)
                nc.scalar.activation(TT[q][4][:], PA[q][:], ACT.Identity, bias=v(LNB),
                                     scale=v(LNG)).then_inc(xn_made[q], 1)
            for h in range(DH):
                for q in QS:
                    act.wait_ge(in_out[q], h + 1)
                    nc.scalar.activation(AB[q][h][:, :, 3:T + 3], (PA, PB)[h][q][:], ACT.Copy).then_inc(xi_copied[q], 1)
            for h in range(DH):
                for q in QS:
                    act.wait_ge(in_out[q], DH + h + 1)
                    nc.scalar.activation(SZ[q][:, h], (PA, PB)[h][q][:], ACT.Tanh).then_inc(z_tanh[q], 1)
            for h in range(DH):
                for q in QS:
                    act.wait_ge(conv[q], DH * (TAPS - 1) + h + 1)
                    nc.scalar.activation(TT[q][h][:], XC[q][:, h], ACT.Tanh).then_inc(c_tanh[q], 1)
            for q in QS:
                act.wait_ge(in_out[q], 5)
                nc.scalar.activation(LOW[q], PA[q][0:RANK], ACT.Copy).then_inc(stacked[q], 1)
                nc.scalar.activation(ST[q][:], PA[q][:], ACT.Copy).then_inc(stacked[q], 1)
            for q in QS:
                act.wait_ge(rest[q], 1)
                nc.scalar.activation(ST[q][64:P], TT[q][2][64:P], ACT.Copy).then_inc(stacked[q], 1)
            for h in range(DH):
                for q in QS:
                    act.wait_ge(in_out[q], 5 + h + 1)
                    nc.scalar.activation(TT[q][h][:], (PB, PA)[h][q][:], ACT.Abs, bias=v(DTB + h)).then_inc(dt_in[q], 1)
                    nc.scalar.activation(TT[q][3 + h][:], (PB, PA)[h][q][:], ACT.Identity,
                                         bias=v(DTB + h)).then_inc(dt_in[q], 1)
            for h in range(DH):
                for q in QS:
                    act.wait_ge(dt_in[q], 2 * h + 1)
                    nc.scalar.activation(TT[q][h][:], TT[q][h][:], ACT.Exp, scale=-1.0).then_inc(dt_exp[q], 1)
            for h in range(DH):
                for q in QS:
                    act.wait_ge(dt_exp[q], h + 1)
                    nc.scalar.activation(TT[q][5 + h][:], TT[q][h][:], ACT.Ln, bias=1.0).then_inc(dt_log[q], 1)

            def unit(q, j, n, s, ring):
                if not (isinstance(n, int) and n < 2):
                    act.wait_ge(scanned[q], n - 1)
                for h in range(DH):
                    nc.scalar.activation(TT[q][ring][:, h, 1:T], DT[q][:, h, j, 1:T], ACT.Exp,
                                         scale=nega[:, bass.ds(NS * h + s, 1)]).then_inc(decayed[q], 1)
                act.wait_ge(c_spread[q], n + 1)
                if not (isinstance(n, int) and n < 2):
                    act.wait_ge(weighed[q], n - 1)
                nc.scalar.activation(CB[q][:, ring, :], bank_c, ACT.Copy).then_inc(c_kept[q], 1)

            act.wait_ge(a_set, 1)
            for q in QS:
                act.wait_ge(dt_pool[q], 4)
                act.wait_ge(zeros_set[q], 2)
                for j in range(2):
                    for s in range(4):
                        unit(q, j, NS * j + s, s, s % 2)
                    with act.Fori(2, NS // 2) as i:
                        for r in range(2):
                            unit(q, j, NS * j + 2 * i + r, 2 * i + r, r)
            ffn_block(1, 4)

        @block.vector
        def _(dve):
            ve = nc.vector
            ve.memset(power[:], -0.5).then_inc(power_set, 1)
            for q in QS:
                ve.memset(H[q][:, :, 0:1], 0.0)
                ve.memset(PP[q][:, :, 0:1], -1e38)
                ve.memset(AB[q][0][:, :, 0:3], 0.0)
                ve.memset(AB[q][1][:, :, 0:3], 0.0).then_inc(pads_set, 1)
            dve.wait_ge(decay_exp, 1)
            ve.tensor_scalar(negw[:], negw[:], -1.0, None, ALU.mult).then_inc(decay_set, 1)
            dve.wait_ge(a_exp, 1)
            ve.tensor_scalar(nega[:], nega[:], -1.0, None, ALU.mult).then_inc(a_set, 1)

            def norm(k, src, ready, value, once=None, twice=None):
                for q in QS:
                    dve.wait_ge(ready[q], value)
                    for n in range(NB):
                        last = ve.bn_stats(stats[q][:, n, :], blocks(src[q])[:, n, :])
                    last.then_inc(stats_made[q], 1)
                for q in QS:
                    dve.wait_ge(stats_made[q], k + 1)
                    for n in range(NB):
                        last = ve.bn_aggr(moments[q][:, n, :], stats[q][:, n, :])
                    last.then_inc(moments_made[q], 1)
                for q in QS:
                    dve.wait_ge(rstd_made[q], k + 1)
                    for n in range(NB):
                        mean = moments[q][:, n, 0:1]
                        if once is not None:
                            ve.tensor_scalar(blocks(once[q])[:, n, :], blocks(src[q])[:, n, :], mean,
                                             rstd[q][:, 0, n:n + 1], ALU.subtract, ALU.mult)
                        last = ve.tensor_scalar(blocks(TT[q][0])[:, n, :], blocks(src[q])[:, n, :], mean,
                                                rstd[q][:, int(once is not None), n:n + 1], ALU.subtract, ALU.mult)
                    last.then_inc(normed[q], 1)

            norm(0, X, x_loaded, 16, once=U)

            def mix(q, dst, col):
                ve.scalar_tensor_tensor(out=TT[q][dst][:], in0=TT[q][3][:], scalar=v(col), in1=H[q][:, :, 0:T],
                                        op0=ALU.mult, op1=ALU.add).then_inc(mixed[q], 1)

            for q in QS:
                dve.wait_ge(h_diff[q], 1)
                mix(q, 4, TMK)
                mix(q, 5, TMV)
                mix(q, 6, TMR)
            dve.wait_ge(decay_set, 1)
            for q in QS:
                dve.wait_ge(kv_copied[q], 1)
                for j in range(2):
                    ve.tensor_tensor_scan(PP[q][:, j, 1:T + 1], negw[:, 0:1].to_broadcast([P, T]), TT[q][0][:, j, :],
                                          -1e38, ALU.add, ALU.max).then_inc(max_run[q], 1)
            for q in QS:
                dve.wait_ge(out_diff[q], 1)
                ve.tensor_scalar(TT[q][0][:], TT[q][6][:], v(FIRST), 0.0, ALU.subtract, ALU.min).then_inc(out_diff[q], 1)
                ve.tensor_scalar(TT[q][6][:], TT[q][6][:], v(FIRST), 0.0, ALU.subtract, ALU.max).then_inc(out_diff[q], 1)
            for q in QS:
                dve.wait_ge(wkv_exp[q], 1)
                dve.wait_ge(wkv_exp[q], 2)
                for j in range(2):
                    ve.tensor_tensor_scan(AB[q][1][:, j, 3:T + 3], TT[q][3][:, j, :], TT[q][4][:, j, :],
                                          0.0, ALU.mult, ALU.add).then_inc(summed[q], 1)
                dve.wait_ge(wkv_step[q], 1)
                for j in range(2):
                    ve.tensor_tensor_scan(AB[q][0][:, j, 3:T + 3], TT[q][3][:, j, :], TT[q][5][:, j, :],
                                          0.0, ALU.mult, ALU.add).then_inc(summed[q], 1)
            for q in QS:
                dve.wait_ge(wkv_step[q], 6)
                ve.reciprocal(TT[q][0][:], TT[q][0][:]).then_inc(den_inv[q], 1)
            for q in QS:
                dve.wait_ge(r_tanh[q], 1)
                dve.wait_ge(wkv_step[q], 7)
                ve.scalar_tensor_tensor(out=TT[q][3][:], in0=TT[q][2][:], scalar=1.0, in1=TT[q][3][:],
                                        op0=ALU.add, op1=ALU.mult).then_inc(r_scaled[q], 1)
            for q in QS:
                dve.wait_ge(projected[q], 4)
                ve.tensor_tensor(U[q][:], PB[q][:], U[q][:], ALU.add).then_inc(x_att[q], 1)
            norm(1, U, x_att, 1)
            for q in QS:
                dve.wait_ge(h_diff[q], 2)
                mix(q, 4, FTMK)
                mix(q, 5, FTMR)
            for q in QS:
                dve.wait_ge(projected[q], 10)
                dve.wait_ge(rec_tanh[q], 1)
                ve.scalar_tensor_tensor(out=TT[q][6][:], in0=TT[q][6][:], scalar=1.0, in1=PB[q][:],
                                        op0=ALU.add, op1=ALU.mult).then_inc(chan[q], 1)
            for q in QS:
                dve.wait_ge(chan[q], 1)
                dve.wait_ge(x_plus[q], 1)
                ve.scalar_tensor_tensor(out=X[q][:], in0=TT[q][6][:], scalar=0.5, in1=X[q][:],
                                        op0=ALU.mult, op1=ALU.add).then_inc(x_ready[q], 1)

            def ffn_block(i, k):
                norm(k, X, x_ready, 2 * i + 1)
                for j in range(HJ):
                    n = HJ * i + j + 1
                    g = (3, 7)[j % 2]
                    for q in QS:
                        dve.wait_ge(gate_tanh[q], n)
                        ve.scalar_tensor_tensor(out=TT[q][g][:], in0=TT[q][g][:], scalar=1.0, in1=PA[q][:],
                                                op0=ALU.add, op1=ALU.mult).then_inc(gated[q], 1)
                    for q in QS:
                        dve.wait_ge(gated[q], n)
                        dve.wait_ge(up_out[q], n)
                        ve.tensor_tensor(TT[q][4 + j][:], PB[q][:], TT[q][g][:], ALU.mult).then_inc(hidden[q], 1)
                for q in QS:
                    dve.wait_ge(down_out[q], i + 1)
                    ve.tensor_tensor(X[q][:], PA[q][:], X[q][:], ALU.add).then_inc(x_ready[q], 1)

            ffn_block(0, 2)
            norm(3, X, x_ready, 2, once=[TT[q][2] for q in QS])
            dve.wait_ge(taps_halved, 1)
            for h in range(DH):
                for q in QS:
                    dve.wait_ge(z_tanh[q], h + 1)
                    ve.scalar_tensor_tensor(out=SZ[q][:, h], in0=SZ[q][:, h], scalar=1.0, in1=(PA, PB)[h][q][:],
                                            op0=ALU.add, op1=ALU.mult).then_inc(z_silu[q], 1)
            for tap in range(TAPS):
                for h in range(DH):
                    for q in QS:
                        w = v(CONVW + TAPS * h + tap)
                        taken = AB[q][h][:, :, tap:tap + T]
                        if tap == 0:
                            dve.wait_ge(xi_copied[q], h + 1)
                            ve.tensor_scalar(XC[q][:, h], taken, w, v(CONVB + h), ALU.mult, ALU.add).then_inc(conv[q], 1)
                        else:
                            dve.wait_ge(conv[q], DH * (tap - 1) + h + 1)
                            ve.scalar_tensor_tensor(out=XC[q][:, h], in0=taken, scalar=w, in1=XC[q][:, h],
                                                    op0=ALU.mult, op1=ALU.add).then_inc(conv[q], 1)
            for h in range(DH):
                for q in QS:
                    dve.wait_ge(c_tanh[q], h + 1)
                    ve.scalar_tensor_tensor(out=XC[q][:, h], in0=TT[q][h][:], scalar=1.0, in1=XC[q][:, h],
                                            op0=ALU.add, op1=ALU.mult).then_inc(xc_made[q], 1)
            for q in QS:
                dve.wait_ge(stacked[q], 2)
                dve.wait_ge(x_plus[q], 2)
                ve.tensor_tensor(TT[q][2][64:P], PA[q][64:P], ST[q][64:P], ALU.subtract).then_inc(rest[q], 1)
            for q in QS:
                dve.wait_ge(stacked[q], 3)
                ve.tensor_tensor(ST[q][96:P], TT[q][2][96:P], ST[q][96:P], ALU.subtract).then_inc(rest[q], 1)
            for h in range(DH):
                for q in QS:
                    dve.wait_ge(dt_exp[q], h + 1)
                    dve.wait_ge(rest[q], 2)
                    ve.tensor_scalar(TT[q][(2, 7)[h]][:], TT[q][h][:], 1.0, 1.0, ALU.add, ALU.subtract).then_inc(dt_vector[q], 1)
            for h in range(DH):
                for q in QS:
                    dve.wait_ge(dt_log[q], h + 1)
                    ve.scalar_tensor_tensor(out=DT[q][:, h], in0=TT[q][3 + h][:], scalar=0.0, in1=TT[q][5 + h][:],
                                            op0=ALU.max, op1=ALU.add).then_inc(dt_vector[q], 1)

            def drive(q, j, n, ring):
                dve.wait_ge(b_spread[q], n + 1)
                if not (isinstance(n, int) and n < 2):
                    dve.wait_ge(scanned[q], n - 1)
                ve.tensor_tensor(TT[q][2 + ring][:], DU[q][:, :, j, :], bank_b.unsqueeze(1).to_broadcast([P, DH, T]),
                                 ALU.mult).then_inc(driven[q], 1)

            def scan(q, n, ring):
                dve.wait_ge(driven[q], n + 1)
                dve.wait_ge(decayed[q], DH * n + DH)
                if not (isinstance(n, int) and n < 2):
                    dve.wait_ge(weighed[q], n - 1)
                ve.tensor_tensor_scan(flat(TT[q][4 + ring]), flat(TT[q][ring]), flat(TT[q][2 + ring]), 0.0,
                                      ALU.mult, ALU.add).then_inc(scanned[q], 1)

            def flat(tile):
                return tile[:].rearrange("p a b -> p (a b)")

            def take_y(q, j):
                dve.wait_ge(y_summed[q], NS * (j + 1))
                for h in range(DH):
                    ve.scalar_tensor_tensor(out=XC[q][:, h, j, :], in0=XC[q][:, h, j, :], scalar=v(SKIP + h),
                                            in1=bank_y[:, h, :], op0=ALU.mult, op1=ALU.add).then_inc(y_taken[q], 1)

            for q in QS:
                dve.wait_ge(dt_pool[q], 6)
                for ring in range(2):
                    ve.memset(TT[q][ring][:, :, 0:1], 0.0).then_inc(zeros_set[q], 1)
            for q in QS:
                for j in range(2):
                    for s in range(4):
                        n = NS * j + s
                        if n == NS + 2:
                            take_y(q, 0)
                        drive(q, j, n, s % 2)
                        if n >= 1:
                            scan(q, n - 1, (s + 1) % 2)
                    with dve.Fori(2, NS // 2) as i:
                        for r in range(2):
                            drive(q, j, NS * j + 2 * i + r, r)
                            scan(q, NS * j + 2 * i + r - 1, (r + 1) % 2)
                scan(q, 2 * NS - 1, 1)
                take_y(q, 1)
            for q in QS:
                dve.wait_ge(o_out[q], 1)
                ve.tensor_tensor(X[q][:], PA[q][:], X[q][:], ALU.add).then_inc(x_ready[q], 1)
            ffn_block(1, 4)

        @block.gpsimd
        def _(pool):
            gp = nc.gpsimd

            def difference(k):
                for q in QS:
                    pool.wait_ge(h_made[q], k)
                    gp.tensor_tensor(TT[q][3][:], H[q][:, :, 1:T + 1], H[q][:, :, 0:T], ALU.subtract).then_inc(h_diff[q], 1)

            def root(k):
                for q in QS:
                    pool.wait_ge(moments_made[q], k + 1)
                    gp.tensor_scalar(rstd[q][:, 0, :], moments[q][:, :, 1], 1.0, EPS, ALU.mult, ALU.add).then_inc(var_eps[q], 1)
                    gp.tensor_scalar(rstd[q][:, 1, :], moments[q][:, :, 1], 1.0 + EPS, EPS * EPS,
                                     ALU.mult, ALU.add).then_inc(var_eps[q], 1)
                for q in QS:
                    pool.wait_ge(var_eps[q], 2 * k + 2)
                    gp.tensor_tensor(rstd[q][:], rstd[q][:], power[:], ALU.pow).then_inc(rstd_made[q], 1)

            pool.wait_ge(power_set, 1)
            root(0)
            difference(1)
            for q in QS:
                pool.wait_ge(max_run[q], 2)
                gp.tensor_tensor(TT[q][3][:], PP[q][:, :, 0:T], PP[q][:, :, 1:T + 1], ALU.subtract).then_inc(max_diff[q], 1)
                gp.tensor_tensor(TT[q][4][:], TT[q][0][:], PP[q][:, :, 1:T + 1], ALU.subtract).then_inc(max_diff[q], 1)
                pool.wait_ge(projected[q], 3)
                gp.tensor_tensor(TT[q][6][:], PP[q][:, :, 0:T], TT[q][0][:], ALU.subtract).then_inc(out_diff[q], 1)
            for q in QS:
                pool.wait_ge(wkv_exp[q], 2)
                pool.wait_ge(kv_copied[q], 2)
                gp.tensor_tensor(TT[q][5][:], TT[q][4][:], TT[q][1][:], ALU.mult).then_inc(wkv_step[q], 1)
            for q in QS:
                pool.wait_ge(wkv_exp[q], 4)
                gp.tensor_tensor(TT[q][1][:], TT[q][6][:], TT[q][1][:], ALU.mult).then_inc(wkv_step[q], 1)
            for q in QS:
                pool.wait_ge(summed[q], 4)
                gp.tensor_tensor(TT[q][3][:], TT[q][0][:], AB[q][0][:, :, 2:T + 2], ALU.mult).then_inc(wkv_step[q], 1)
                gp.tensor_tensor(TT[q][0][:], TT[q][0][:], AB[q][1][:, :, 2:T + 2], ALU.mult).then_inc(wkv_step[q], 1)
                pool.wait_ge(wkv_step[q], 3)
                gp.tensor_tensor(TT[q][3][:], TT[q][3][:], TT[q][1][:], ALU.add).then_inc(wkv_step[q], 1)
                pool.wait_ge(wkv_step[q], 4)
                gp.tensor_tensor(TT[q][0][:], TT[q][0][:], TT[q][6][:], ALU.add).then_inc(wkv_step[q], 1)
            for q in QS:
                pool.wait_ge(den_inv[q], 1)
                pool.wait_ge(wkv_step[q], 5)
                gp.tensor_tensor(TT[q][3][:], TT[q][3][:], TT[q][0][:], ALU.mult).then_inc(wkv_step[q], 1)
            root(1)
            for q in QS:
                pool.wait_ge(x_att[q], 1)
                gp.tensor_tensor(X[q][:], X[q][:], U[q][:], ALU.add).then_inc(x_plus[q], 1)
            difference(2)
            for j in range(RJ):
                for q in QS:
                    pool.wait_ge(relu[q], j + 1)
                    gp.tensor_tensor(TT[q][j][:], TT[q][j][:], TT[q][j][:], ALU.mult).then_inc(key_sq[q], 1)
            root(2)
            root(3)
            for q in QS:
                pool.wait_ge(normed[q], 4)
                gp.tensor_tensor(X[q][:], X[q][:], TT[q][2][:], ALU.add).then_inc(x_plus[q], 1)
            for h in range(DH):
                for q in QS:
                    pool.wait_ge(dt_vector[q], h + 1)
                    pool.wait_ge(dt_log[q], h + 1)
                    gp.tensor_tensor(TT[q][h][:], TT[q][h][:], TT[q][(2, 7)[h]][:], ALU.subtract).then_inc(dt_pool[q], 1)
            for h in range(DH):
                for q in QS:
                    pool.wait_ge(dt_vector[q], 2 + h + 1)
                    pool.wait_ge(dt_pool[q], h + 1)
                    gp.tensor_tensor(DT[q][:, h], DT[q][:, h], TT[q][h][:], ALU.add).then_inc(dt_pool[q], 1)
            for h in range(DH):
                for q in QS:
                    pool.wait_ge(dt_pool[q], 2 + h + 1)
                    gp.tensor_tensor(DU[q][:, h], DT[q][:, h], XC[q][:, h], ALU.mult).then_inc(dt_pool[q], 1)

            def weigh(q, n, ring):
                pool.wait_ge(scanned[q], n + 1)
                pool.wait_ge(c_kept[q], n + 1)
                if not (isinstance(n, int) and n < 2):
                    pool.wait_ge(y_summed[q], n - 1)
                gp.tensor_tensor(TT[q][6 + ring][:], TT[q][4 + ring][:],
                                 CB[q][:, ring, :].unsqueeze(1).to_broadcast([P, DH, T]), ALU.mult).then_inc(weighed[q], 1)

            for q in QS:
                for j in range(2):
                    for s in range(4):
                        weigh(q, NS * j + s, s % 2)
                    with pool.Fori(2, NS // 2) as i:
                        for r in range(2):
                            weigh(q, NS * j + 2 * i + r, r)
            for h in range(DH):
                for q in QS:
                    pool.wait_ge(y_taken[q], 4)
                    pool.wait_ge(z_silu[q], 2)
                    gp.tensor_tensor(XC[q][:, h], XC[q][:, h], SZ[q][:, h], ALU.mult).then_inc(y_gated[q], 1)
            root(4)


def kernel(**inputs):
    import ml_dtypes
    import numpy as np
    import concourse.bacc as bacc
    from concourse.bass_utils import run_bass_kernel_spmd

    a = {k: np.asarray(x) for k, x in inputs.items()}

    def A(k):
        return a["L0_attn_a_" + k]

    def M(k):
        return a["L0_attn_b_" + k]

    def halves(w):
        return w.reshape(DH, P, -1).transpose(1, 0, 2)

    vecs = [A(k)[:, None] for k in ("ln1_w", "ln1_b", "ln2_w", "ln2_b", "time_decay", "time_first", "tmk", "tmv", "tmr",
                                    "f_tmk", "f_tmr")]
    vecs += [M("ln_w")[:, None], M("ln_b")[:, None], halves(M("conv_w")).reshape(P, -1)]
    vecs += [halves(M(k)).reshape(P, -1) for k in ("conv_b", "dt_proj_b", "D_skip", "A_log")]
    xp = halves(M("x_proj_w"))
    bc = xp[:, :, RANK:]
    gap = np.zeros((P, DH, 32 - RANK), xp.dtype)
    down = a["L0_ffn_w_down"].T.reshape(HJ, P, C).transpose(1, 0, 2).reshape(P, HID)
    eye = np.eye(P, dtype=np.float32)
    pick = np.zeros((P, 2 * NS, P), ml_dtypes.bfloat16)
    for s in range(2 * NS):
        pick[[32 + s, 64 + s, 96 + s], s, :] = 1
    arrays = {
        "x": A("x").reshape(B * T, C),
        "vec": np.concatenate(vecs, 1),
        "att": np.stack([A(k).T for k in ("att_kw", "att_vw", "att_rw", "att_ow")], 1),
        "fkw": A("f_kw").T,
        "frw": A("f_rw").T,
        "fvw": A("f_vw").T.reshape(RJ, P, C).transpose(1, 0, 2),
        "ffn": np.stack([a["L0_ffn_w_gate"].T, a["L0_ffn_w_up"].T, down], 1),
        "inp": M("in_proj_w"),
        "xpj": np.concatenate([xp[:, :, :RANK], gap, bc, bc, bc], 2),
        "dtw": M("dt_proj_w"),
        "outp": halves(M("out_proj_w")),
        "mat": eye,
        "sel": pick,
    }
    arrays = {f"in_{k}_dram": np.ascontiguousarray(x) for k, x in arrays.items()}
    nc = bacc.Bacc("TRN2", target_bir_lowering=False, num_devices=1)
    args = [nc.dram_tensor(k, x.shape, mybir.dt.from_np(x.dtype), kind="ExternalInput").ap() for k, x in arrays.items()]
    out = nc.dram_tensor("out_dram", (B * T, C), F32, kind="ExternalOutput").ap()
    build(nc, *args, out)
    r = run_bass_kernel_spmd(nc, [arrays], core_ids=[0])
    y = r.results[0]["out_dram"]
    return y.reshape(B, T, C)
```

```python
from contextlib import ExitStack

import concourse.bass as bass
from concourse import mybir

ALU = mybir.AluOpType
ACT = mybir.ActivationFunctionType
F32 = mybir.dt.float32
BF16 = mybir.dt.bfloat16
I32 = mybir.dt.int32

P = 128
B, T, C = 4, 512, 128
NB = T // P
RF = 512
RJ = RF // P
HID = 384
HJ = HID // P
DI = 256
DH = DI // P
RANK, NS, TAPS = 8, 16, 4
RING = 4
LAG = 3
EPS = 1e-5
WSCALE = 1.0 / 127.0

LN1G, LN1B, LN2G, LN2B, DECAY, FIRST, TMK, TMV, TMR, FTMK, FTMR, LNG, LNB = range(13)
CONVW = 13
CONVB = CONVW + DH * TAPS
DTB = CONVB + DH
SKIP = DTB + DH
ALOG = SKIP + DH
NVEC = ALOG + DH * NS


def nth(k, q):
    return B * (k - 1) + q + 1


def build(nc, x_in, vec_in, att_in, fkw_in, frw_in, fvw_in, ffn_in, inp_in, xpj_in, dtw_in, outp_in,
          ident_in, sel_in, out):
    with ExitStack() as ctx:
        def sb(name, shape, dt=F32):
            return ctx.enter_context(nc.sbuf_tensor(name, shape, dt))

        def sem(name):
            return ctx.enter_context(nc.semaphore(name))

        vec = sb("vec", [P, NVEC])
        att = sb("att", [P, 4, C])
        fkw = sb("fkw", [P, RF])
        frw = sb("frw", [P, C])
        fvw = sb("fvw", [P, RJ, C])
        ffn = sb("ffn", [P, 3, HID])
        ffn_int = sb("ffn_int", [P, 3, HID], I32)
        inp = sb("inp", [P, 2 * DI])
        xpj = sb("xpj", [P, DH, P])
        dtw = sb("dtw", [RANK, DI])
        outp = sb("outp", [P, DH, C])
        eye = sb("eye", [P, P])
        sel = sb("sel", [P, 2 * NS, P], BF16)
        negw = sb("negw", [P, 1])
        nega = sb("nega", [P, DH * NS])
        power = sb("power", [P, 2, NB])
        ident = eye[:, :]

        QS = range(B)
        stats = [sb(f"stats{q}", [P, NB, 6]) for q in QS]
        moments = [sb(f"moments{q}", [P, NB, 2]) for q in QS]
        rstd = [sb(f"rstd{q}", [P, 2, NB]) for q in QS]
        X = [sb(f"X{q}", [P, T]) for q in QS]
        U = [sb(f"U{q}", [P, T]) for q in QS]
        H = [sb(f"H{q}", [P, T + 1]) for q in QS]
        PP = [sb(f"PP{q}", [P, T + 1]) for q in QS]
        XI = [sb(f"XI{q}", [P, DH, T + 3]) for q in QS]
        XC = [sb(f"XC{q}", [P, DH, T]) for q in QS]
        SZ = [sb(f"SZ{q}", [P, DH, T]) for q in QS]
        DT = [sb(f"DT{q}", [P, DH, T]) for q in QS]
        DU = [sb(f"DU{q}", [P, DH, T]) for q in QS]
        SCR = sb("SCR", [P, 8 * B, T])

        def tile(q, i):
            return SCR[:, 8 * q + i, :]

        def tiles(q, i):
            return SCR[:, 8 * q + i:8 * q + i + 2, :]

        AA = [XI[q][:, 0, :] for q in QS]
        BB = [XI[q][:, 1, :] for q in QS]
        ST = [H[q][:, 0:T // 2].bitcast(BF16) for q in QS]
        LOW = [tile(q, 7)[0:RANK] for q in QS]

        PS = [ctx.enter_context(nc.psum_tensor(f"PS{q}", [P, 2, T], F32)) for q in QS]
        PA, PB = [PS[q][:, 0, :] for q in QS], [PS[q][:, 1, :] for q in QS]

        decay_ring = [SCR[:, 2 * r:2 * r + 2, :] for r in range(RING)]
        drive_ring = [SCR[:, 2 * (RING + r):2 * (RING + r) + 2, :] for r in range(RING)]
        state_ring = [SCR[:, 2 * (2 * RING + r):2 * (2 * RING + r) + 2, :] for r in range(RING)]
        term_ring = [SCR[:, 2 * (3 * RING + r):2 * (3 * RING + r) + 2, :] for r in range(RING)]
        c_ring = [PP[r][:, 0:T] for r in range(RING)]
        bank_y = [PS[0], PS[1]]
        bank_b, bank_c = PS[2], PS[3]

        loaded_v, loaded_m, loaded_a, loaded_f, loaded_q, loaded_s = (
            sem(n) for n in ("loaded_v", "loaded_m", "loaded_a", "loaded_f", "loaded_q", "loaded_s"))
        x_loaded, out_stored = [sem(f"x_loaded{q}") for q in QS], sem("out_stored")
        power_set, pads_set, decay_exp, decay_set, a_exp, a_set, dequantised, out_halved, z_halved, taps_halved = (
            sem(n) for n in ("power_set", "pads_set", "decay_exp", "decay_set", "a_exp", "a_set", "dequantised",
                             "out_halved", "z_halved", "taps_halved"))
        stats_made, moments_made, var_eps, rstd_made, normed, turned = (
            sem(n) for n in ("stats_made", "moments_made", "var_eps", "rstd_made", "normed", "turned"))
        h_made, h_diff, mixed = sem("h_made"), sem("h_diff"), sem("mixed")
        kvr_out, kv_copied, r_tanh, max_run, max_diff, out_diff, out_bound, wkv_exp = (
            sem(n) for n in ("kvr_out", "kv_copied", "r_tanh", "max_run", "max_diff", "out_diff", "out_bound", "wkv_exp"))
        v_weighed, b_summed, a_summed, prior, num_kept, den_made, den_inv, num_made, num_scaled, wkv_made, att_out = (
            sem(n) for n in ("v_weighed", "b_summed", "a_summed", "prior", "num_kept", "den_made", "den_inv", "num_made",
                             "num_scaled", "wkv_made", "att_out"))
        x_att, x_plus, keys_out, relu, key_sq, rec_out, rec_tanh, val_out, chan, x_ready = (
            sem(n) for n in ("x_att", "x_plus", "keys_out", "relu", "key_sq", "rec_out", "rec_tanh", "val_out",
                             "chan", "x_ready"))
        hn_made, gate_out, gate_tanh, gated, up_out, hidden, down_out = (
            sem(n) for n in ("hn_made", "gate_out", "gate_tanh", "gated", "up_out", "hidden", "down_out"))
        xn_made, xi_out, conv_begun, z_out, z_tanh, z_silu, conv, c_tanh, xc_made = (
            sem(n) for n in ("xn_made", "xi_out", "conv_begun", "z_out", "z_tanh", "z_silu", "conv", "c_tanh", "xc_made"))
        xp_out, low_made, stack1, rest1, stack2, stack3, dt_out, dt_in = (
            sem(n) for n in ("xp_out", "low_made", "stack1", "rest1", "stack2", "stack3", "dt_out", "dt_in"))
        dt_exp, dt_log, dt_round, dt_rest, dt_log1p, dt_made, du_made = (
            sem(n) for n in ("dt_exp", "dt_log", "dt_round", "dt_rest", "dt_log1p", "dt_made", "du_made"))
        zeros_set, b_spread, c_spread, c_kept, decayed, driven, scanned, weighed, y_summed, y_taken = (
            sem(n) for n in ("zeros_set", "b_spread", "c_spread", "c_kept", "decayed", "driven", "scanned",
                             "weighed", "y_summed", "y_taken"))
        y_gated, o_out = sem("y_gated"), sem("o_out")

        x_view = x_in.rearrange("(q n p) c -> q p n c", q=B, p=P)
        out_view = out.rearrange("(q n p) c -> q p n c", q=B, p=P)

        def blocks(t):
            return t.rearrange("p (n c) -> p n c", c=P)

        def v(col, n=1):
            return vec[:, col:col + n]

        def flat(t):
            return t.rearrange("p a b -> p (a b)")

        def old(n, back):
            return not isinstance(n, int) or n >= back

        block = ctx.enter_context(nc.Block())

        @block.sync
        def _(sp):
            sp.dma_start(blocks(X[0][:, :]), x_view[0]).then_inc(x_loaded[0], 16)
            sp.dma_start(blocks(X[1][:, :]), x_view[1]).then_inc(x_loaded[1], 16)
            sp.dma_start(eye[:], ident_in).then_inc(loaded_m, 16)
            sp.dma_start(att[:], att_in).then_inc(loaded_a, 16)
            sp.dma_start(fkw[:], fkw_in).then_inc(loaded_f, 16)
            sp.dma_start(frw[:], frw_in).then_inc(loaded_f, 16)
            sp.dma_start(fvw[:], fvw_in).then_inc(loaded_f, 16)
            sp.dma_start(inp[:], inp_in).then_inc(loaded_s, 16)
            sp.dma_start(xpj[:], xpj_in).then_inc(loaded_s, 16)
            sp.dma_start(dtw[:], dtw_in).then_inc(loaded_s, 16)
            sp.dma_start(outp[:], outp_in).then_inc(loaded_s, 16)
            sp.dma_start(sel[:], sel_in).then_inc(loaded_s, 16)
            for q in QS:
                sp.wait_ge(x_ready, nth(4, q))
                sp.dma_start(out_view[q], blocks(X[q][:, :])).then_inc(out_stored, 16)
            sp.wait_ge(out_stored, 16 * B)

        @block.tensor
        def _(pe):
            mm = nc.tensor.matmul

            def turn(k):
                for q in QS:
                    pe.wait_ge(normed, nth(k, q))
                    for n in range(NB):
                        last = nc.tensor.transpose(blocks(PA[q])[:, n, :], blocks(tile(q, 0))[:, n, :], ident)
                    last.then_inc(turned, 1)

            def back(dst, weights, srcs):
                for n in range(NB):
                    for j, (w, src) in enumerate(zip(weights, srcs)):
                        last = mm(blocks(dst)[:, n, :], blocks(src)[:, n, :], w, start=(j == 0),
                                  stop=(j == len(srcs) - 1), skip_group_check=True)
                return last

            pe.wait_ge(loaded_m, 16)
            turn(1)
            pe.wait_ge(loaded_a, 16)
            for q in QS:
                pe.wait_ge(mixed, nth(1, q))
                mm(PA[q], att[:, 0, :], tile(q, 2), start=True, stop=True).then_inc(kvr_out, 1)
            for q in QS:
                pe.wait_ge(mixed, nth(2, q))
                mm(PB[q], att[:, 1, :], tile(q, 3), start=True, stop=True).then_inc(kvr_out, 1)
            for q in QS:
                pe.wait_ge(mixed, nth(3, q))
                pe.wait_ge(kv_copied, nth(1, q))
                mm(PA[q], att[:, 2, :], tile(q, 4), start=True, stop=True).then_inc(kvr_out, 1)
            pe.wait_ge(out_halved, 1)
            for q in QS:
                pe.wait_ge(wkv_made, nth(1, q))
                back(PB[q], [att[:, 3, :]], [tile(q, 6)]).then_inc(att_out, 1)
            turn(2)
            pe.wait_ge(loaded_f, 48)
            for j in range(0, RJ, 2):
                for q in QS:
                    if j == 0:
                        pe.wait_ge(mixed, nth(4, q))
                    else:
                        pe.wait_ge(relu, nth(1, q))
                    mm(PA[q], fkw[:, j * P:(j + 1) * P], tile(q, 2), start=True, stop=True)
                    mm(PB[q], fkw[:, (j + 1) * P:(j + 2) * P], tile(q, 2), start=True, stop=True).then_inc(keys_out, 1)
            for q in QS:
                pe.wait_ge(mixed, nth(5, q))
                pe.wait_ge(relu, nth(2, q))
                back(PA[q], [frw[:, :]], [tile(q, 3)]).then_inc(rec_out, 1)
            for q in QS:
                pe.wait_ge(key_sq, nth(2, q))
                back(PB[q], [fvw[:, j, :] for j in range(RJ)], [tile(q, 4 + j) for j in range(RJ)]).then_inc(val_out, 1)

            def ffn_block(i, k):
                turn(k)
                pe.wait_ge(dequantised, 3)
                for j in range(HJ):
                    n = HJ * i + j
                    for q in QS:
                        if j == 0:
                            pe.wait_ge(hn_made, nth(i + 1, q))
                        else:
                            pe.wait_ge(gated, nth(n, q))
                        mm(PA[q], ffn[:, 0, j * P:(j + 1) * P], tile(q, 1), start=True, stop=True).then_inc(gate_out, 1)
                        if j > 0:
                            pe.wait_ge(hidden, nth(n, q))
                        mm(PB[q], ffn[:, 1, j * P:(j + 1) * P], tile(q, 1), start=True, stop=True).then_inc(up_out, 1)
                for q in QS:
                    pe.wait_ge(hidden, nth(HJ * (i + 1), q))
                    back(PA[q], [ffn[:, 2, j * P:(j + 1) * P] for j in range(HJ)],
                         [tile(q, 4 + j) for j in range(HJ)]).then_inc(down_out, 1)

            ffn_block(0, 3)
            turn(4)
            pe.wait_ge(loaded_s, 80)
            for q in QS:
                pe.wait_ge(xn_made, nth(1, q))
                mm(PA[q], inp[:, 0:P], tile(q, 2), start=True, stop=True)
                mm(PB[q], inp[:, P:2 * P], tile(q, 2), start=True, stop=True).then_inc(xi_out, 1)
            pe.wait_ge(z_halved, 1)
            for q in QS:
                pe.wait_ge(conv_begun, nth(1, q))
                mm(PA[q], inp[:, 2 * P:3 * P], tile(q, 2), start=True, stop=True)
                mm(PB[q], inp[:, 3 * P:4 * P], tile(q, 2), start=True, stop=True).then_inc(z_out, 1)
            for q in QS:
                pe.wait_ge(z_silu, nth(1, q))
                pe.wait_ge(xc_made, nth(1, q))
                mm(PA[q], xpj[:, 0, :], XC[q][:, 0, :], start=True, stop=False)
                mm(PA[q], xpj[:, 1, :], XC[q][:, 1, :], start=False, stop=True).then_inc(xp_out, 1)
            for q in QS:
                pe.wait_ge(low_made, nth(1, q))
                mm(PB[q], dtw[:, P:DI], LOW[q], start=True, stop=True)
                pe.wait_ge(rest1, nth(1, q))
                mm(PA[q], dtw[:, 0:P], LOW[q], start=True, stop=True).then_inc(dt_out, 1)

            def spread(g, n, s, r):
                if old(n, 2):
                    pe.wait_ge(driven, n - 1)
                mm(bank_b[:, r % 2, :], sel[:, s, :], ST[g], start=True, stop=True).then_inc(b_spread, 1)
                if old(n, 2):
                    pe.wait_ge(c_kept, n - 1)
                mm(bank_c[:, r % 2, :], sel[:, NS + s, :], ST[g], start=True, stop=True).then_inc(c_spread, 1)

            def total(g, n, r, start=False, stop=False):
                pe.wait_ge(weighed, n + 1)
                for h in range(DH):
                    last = mm(bank_y[g % 2][:, h, :], ident, term_ring[r][:, h, :], start=start, stop=stop,
                              skip_group_check=True)
                last.then_inc(y_summed, 1)

            pe.wait_ge(stack3, B)
            pe.wait_ge(dt_in, B)
            for g in QS:
                for s in range(RING):
                    n = NS * g + s
                    spread(g, n, s, s)
                    if n >= LAG:
                        if s == LAG and g >= 2:
                            pe.wait_ge(y_taken, g - 1)
                        total(g if s >= LAG else g - 1, n - LAG, (s - LAG) % RING, start=(s == LAG), stop=(s == LAG - 1))
                with pe.Fori(1, NS // RING) as i:
                    for r in range(RING):
                        spread(g, NS * g + RING * i + r, RING * i + r, r)
                        total(g, NS * g + RING * i + r - LAG, (r - LAG) % RING)
            for d in range(LAG):
                n = NS * B - LAG + d
                total(B - 1, n, n % RING, stop=(d == LAG - 1))

            for q in QS:
                pe.wait_ge(y_gated, q + 1)
                if q < 2:
                    pe.wait_ge(y_taken, B - 1 + q)
                elif q == 2:
                    pe.wait_ge(driven, NS * B)
                else:
                    pe.wait_ge(c_kept, NS * B)
                back(PA[q], [outp[:, h, :] for h in range(DH)], [XC[q][:, h, :] for h in range(DH)]).then_inc(o_out, 1)
            ffn_block(1, 5)

        @block.scalar
        def _(act):
            activation = nc.scalar.activation
            act.dma_start(vec[:], vec_in).then_inc(loaded_v, 16)
            act.dma_start(blocks(X[2][:, :]), x_view[2]).then_inc(x_loaded[2], 16)
            act.dma_start(blocks(X[3][:, :]), x_view[3]).then_inc(x_loaded[3], 16)
            act.dma_start(ffn_int[:], ffn_in).then_inc(loaded_q, 16)
            act.wait_ge(loaded_v, 16)
            activation(negw[:], v(DECAY), ACT.Exp).then_inc(decay_exp, 1)
            activation(nega[:], v(ALOG, DH * NS), ACT.Exp).then_inc(a_exp, 1)
            activation(v(CONVW, DH * TAPS + DH), v(CONVW, DH * TAPS + DH), ACT.Copy, scale=0.5).then_inc(taps_halved, 1)

            act.wait_ge(pads_set, 1)
            for q in QS:
                act.wait_ge(turned, nth(1, q))
                activation(H[q][:, 1:T + 1], PA[q], ACT.Identity, bias=v(LN1B), scale=v(LN1G)).then_inc(h_made, 1)
            for q in QS:
                act.wait_ge(kvr_out, nth(1, q))
                activation(tile(q, 5), PA[q], ACT.Copy).then_inc(kv_copied, 1)
            for q in QS:
                act.wait_ge(kvr_out, nth(2, q))
                activation(tile(q, 6), PB[q], ACT.Copy).then_inc(kv_copied, 1)
            for q in QS:
                act.wait_ge(kvr_out, nth(3, q))
                activation(tile(q, 7), PA[q], ACT.Tanh, scale=0.5).then_inc(r_tanh, 1)
            act.wait_ge(decay_set, 1)
            for q in QS:
                act.wait_ge(max_diff, nth(1, q))
                activation(tile(q, 0), tile(q, 0), ACT.Exp, bias=negw[:, 0:1]).then_inc(wkv_exp, 1)
            for q in QS:
                act.wait_ge(max_diff, nth(2, q))
                activation(tile(q, 1), tile(q, 1), ACT.Exp).then_inc(wkv_exp, 1)
            for q in QS:
                act.wait_ge(out_bound, nth(1, q))
                activation(tile(q, 3), tile(q, 3), ACT.Exp).then_inc(wkv_exp, 1)
            for q in QS:
                act.wait_ge(out_bound, nth(2, q))
                activation(tile(q, 2), tile(q, 2), ACT.Exp, scale=-1.0).then_inc(wkv_exp, 1)
            act.wait_ge(loaded_a, 16)
            activation(att[:, 3, :], att[:, 3, :], ACT.Copy, scale=0.5).then_inc(out_halved, 1)
            act.wait_ge(loaded_s, 80)
            activation(inp[:, DI:2 * DI], inp[:, DI:2 * DI], ACT.Copy, scale=0.5).then_inc(z_halved, 1)
            act.wait_ge(loaded_q, 16)
            for m in range(3):
                activation(ffn[:, m, :], ffn_int[:, m, :], ACT.Copy,
                           scale=WSCALE * 0.5 if m == 0 else WSCALE).then_inc(dequantised, 1)
            for q in QS:
                act.wait_ge(turned, nth(2, q))
                activation(H[q][:, 1:T + 1], PA[q], ACT.Identity, bias=v(LN2B), scale=v(LN2G)).then_inc(h_made, 1)
            for m in range(RJ // 2):
                for q in QS:
                    act.wait_ge(keys_out, nth(m + 1, q))
                    activation(tiles(q, 4 + 2 * m), PS[q][:], ACT.Relu).then_inc(relu, 1)
                for q in QS:
                    act.wait_ge(relu, nth(m + 1, q))
                    activation(tiles(q, 4 + 2 * m), tiles(q, 4 + 2 * m), ACT.Square).then_inc(key_sq, 1)
            for q in QS:
                act.wait_ge(rec_out, nth(1, q))
                activation(tile(q, 0), PA[q], ACT.Tanh, scale=0.5).then_inc(rec_tanh, 1)

            def ffn_block(i, k):
                for q in QS:
                    act.wait_ge(turned, nth(k, q))
                    activation(tile(q, 1), PA[q], ACT.Copy).then_inc(hn_made, 1)
                for j in range(HJ):
                    n = HJ * i + j + 1
                    for q in QS:
                        act.wait_ge(gate_out, nth(n, q))
                        if j == 2:
                            act.wait_ge(hidden, nth(n - 2, q))
                        activation(tile(q, 2 + j % 2), PA[q], ACT.Tanh).then_inc(gate_tanh, 1)

            ffn_block(0, 3)
            for q in QS:
                act.wait_ge(turned, nth(4, q))
                activation(tile(q, 2), PA[q], ACT.Identity, bias=v(LNB), scale=v(LNG)).then_inc(xn_made, 1)
            for q in QS:
                act.wait_ge(xi_out, nth(1, q))
                activation(XI[q][:, :, 3:T + 3], PS[q][:], ACT.Copy)
                for h in range(DH):
                    last = activation(XC[q][:, h, :], PS[q][:, h, :], ACT.Identity, bias=v(CONVB + h),
                                      scale=v(CONVW + TAPS * h + TAPS - 1))
                last.then_inc(conv_begun, 1)
            for q in QS:
                act.wait_ge(z_out, nth(1, q))
                activation(SZ[q][:], PS[q][:], ACT.Tanh).then_inc(z_tanh, 1)
            for q in QS:
                act.wait_ge(conv, nth(TAPS - 1, q))
                activation(tiles(q, 4), XC[q][:], ACT.Tanh).then_inc(c_tanh, 1)
            for q in QS:
                act.wait_ge(xp_out, nth(1, q))
                activation(LOW[q], PA[q][0:RANK], ACT.Copy).then_inc(low_made, 1)
                activation(ST[q], PA[q], ACT.Copy).then_inc(stack1, 1)
            for q in QS:
                act.wait_ge(rest1, nth(1, q))
                activation(ST[q][64:P], tile(q, 6)[64:P], ACT.Copy).then_inc(stack2, 1)
            for q in QS:
                act.wait_ge(dt_out, nth(1, q))
                act.wait_ge(x_plus, nth(2, q))
                for h in range(DH):
                    activation(tile(q, h), PS[q][:, h, :], ACT.Abs, bias=v(DTB + h))
                    last = activation(tile(q, 2 + h), PS[q][:, h, :], ACT.Identity, bias=v(DTB + h))
                last.then_inc(dt_in, 1)
            for q in QS:
                act.wait_ge(dt_in, nth(1, q))
                activation(tiles(q, 0), tiles(q, 0), ACT.Exp, scale=-1.0).then_inc(dt_exp, 1)
            for q in QS:
                act.wait_ge(dt_exp, nth(1, q))
                activation(tiles(q, 4), tiles(q, 0), ACT.Ln, bias=1.0).then_inc(dt_log, 1)

            def unit(g, n, s, r):
                act.wait_ge(c_spread, n + 1)
                if old(n, RING):
                    act.wait_ge(weighed, n - RING + 1)
                activation(c_ring[r], bank_c[:, r % 2, :], ACT.Copy).then_inc(c_kept, 1)
                if old(n, RING):
                    act.wait_ge(scanned, n - RING + 1)
                for h in range(DH):
                    last = activation(decay_ring[r][:, h, 1:T], DT[g][:, h, 1:T], ACT.Exp,
                                      scale=nega[:, bass.ds(NS * h + s, 1)])
                last.then_inc(decayed, 1)

            act.wait_ge(a_set, 1)
            act.wait_ge(du_made, B)
            act.wait_ge(zeros_set, 1)
            for g in QS:
                for s in range(RING):
                    unit(g, NS * g + s, s, s)
                with act.Fori(1, NS // RING) as i:
                    for r in range(RING):
                        unit(g, NS * g + RING * i + r, RING * i + r, r)
            ffn_block(1, 5)

        @block.vector
        def _(dve):
            ve = nc.vector
            ve.memset(power[:], -0.5).then_inc(power_set, 1)
            for q in QS:
                ve.memset(H[q][:, 0:1], 0.0)
                ve.memset(PP[q][:, 0:1], -1e38)
                last = ve.memset(XI[q][:, :, 0:3], 0.0)
            last.then_inc(pads_set, 1)

            def norm(k, src, ready, once=None):
                for q in QS:
                    dve.wait_ge(*ready(q))
                    for n in range(NB):
                        last = ve.bn_stats(stats[q][:, n, :], blocks(src[q])[:, n, :])
                    last.then_inc(stats_made, 1)
                for q in QS:
                    dve.wait_ge(stats_made, nth(k, q))
                    for n in range(NB):
                        last = ve.bn_aggr(moments[q][:, n, :], stats[q][:, n, :])
                    last.then_inc(moments_made, 1)
                for q in QS:
                    dve.wait_ge(rstd_made, nth(k, q))
                    for n in range(NB):
                        mean = moments[q][:, n, 0:1]
                        if once is not None:
                            ve.tensor_scalar(blocks(once[q])[:, n, :], blocks(src[q])[:, n, :], mean,
                                             rstd[q][:, 0, n:n + 1], ALU.subtract, ALU.mult)
                        last = ve.tensor_scalar(blocks(tile(q, 0))[:, n, :], blocks(src[q])[:, n, :], mean,
                                                rstd[q][:, int(once is not None), n:n + 1], ALU.subtract, ALU.mult)
                    last.then_inc(normed, 1)

            XS, US = [X[q][:, :] for q in QS], [U[q][:, :] for q in QS]
            norm(1, XS, lambda q: (x_loaded[q], 16), once=US)
            dve.wait_ge(decay_exp, 1)
            ve.tensor_scalar(negw[:], negw[:], -1.0, None, ALU.mult).then_inc(decay_set, 1)
            dve.wait_ge(a_exp, 1)
            ve.tensor_scalar(nega[:], nega[:], -1.0, None, ALU.mult).then_inc(a_set, 1)

            def mix(k, i, dst, col):
                for q in QS:
                    dve.wait_ge(h_diff, nth(i, q))
                    ve.scalar_tensor_tensor(out=tile(q, dst), in0=tile(q, 1), scalar=v(col), in1=H[q][:, 0:T],
                                            op0=ALU.mult, op1=ALU.add).then_inc(mixed, 1)

            mix(1, 1, 2, TMK)
            mix(2, 1, 3, TMV)
            mix(3, 1, 4, TMR)
            dve.wait_ge(decay_set, 1)
            for q in QS:
                dve.wait_ge(kv_copied, nth(1, q))
                ve.tensor_tensor_scan(PP[q][:, 1:T + 1], negw[:, 0:1].to_broadcast([P, T]), tile(q, 5),
                                      -1e38, ALU.add, ALU.max).then_inc(max_run, 1)
            for q in QS:
                dve.wait_ge(max_run, nth(1, q))
                ve.scalar_tensor_tensor(out=tile(q, 2), in0=PP[q][:, 0:T], scalar=v(FIRST), in1=tile(q, 5),
                                        op0=ALU.subtract, op1=ALU.subtract).then_inc(out_diff, 1)
            for q in QS:
                dve.wait_ge(out_diff, nth(1, q))
                dve.wait_ge(kv_copied, nth(2, q))
                ve.tensor_scalar(tile(q, 3), tile(q, 2), 0.0, None, ALU.min).then_inc(out_bound, 1)
            for q in QS:
                dve.wait_ge(out_bound, nth(1, q))
                ve.tensor_scalar(tile(q, 2), tile(q, 2), 0.0, None, ALU.max).then_inc(out_bound, 1)
            for q in QS:
                dve.wait_ge(wkv_exp, nth(2, q))
                ve.tensor_tensor_scan(BB[q][:, 3:T + 3], tile(q, 0), tile(q, 1), 0.0,
                                      ALU.mult, ALU.add).then_inc(b_summed, 1)
            for q in QS:
                dve.wait_ge(v_weighed, nth(1, q))
                ve.tensor_tensor_scan(AA[q][:, 3:T + 3], tile(q, 0), tile(q, 4), 0.0,
                                      ALU.mult, ALU.add).then_inc(a_summed, 1)
            for q in QS:
                dve.wait_ge(prior, nth(2, q))
                ve.tensor_tensor(tile(q, 6), tile(q, 1), tile(q, 6), ALU.add).then_inc(num_made, 1)
            for q in QS:
                dve.wait_ge(den_made, nth(1, q))
                ve.reciprocal(tile(q, 3), tile(q, 3)).then_inc(den_inv, 1)
                dve.wait_ge(num_made, nth(1, q))
                dve.wait_ge(r_tanh, nth(1, q))
                ve.scalar_tensor_tensor(out=tile(q, 6), in0=tile(q, 7), scalar=1.0, in1=tile(q, 6),
                                        op0=ALU.add, op1=ALU.mult).then_inc(num_scaled, 1)
                dve.wait_ge(den_inv, nth(1, q))
                dve.wait_ge(num_scaled, nth(1, q))
                ve.tensor_tensor(tile(q, 6), tile(q, 6), tile(q, 3), ALU.mult).then_inc(wkv_made, 1)
            for q in QS:
                dve.wait_ge(att_out, nth(1, q))
                ve.tensor_tensor(US[q], PB[q], US[q], ALU.add).then_inc(x_att, 1)
            norm(2, US, lambda q: (x_att, nth(1, q)))
            mix(4, 2, 2, FTMK)
            mix(5, 2, 3, FTMR)
            for q in QS:
                dve.wait_ge(val_out, nth(1, q))
                dve.wait_ge(rec_tanh, nth(1, q))
                ve.scalar_tensor_tensor(out=tile(q, 0), in0=tile(q, 0), scalar=1.0, in1=PB[q],
                                        op0=ALU.add, op1=ALU.mult).then_inc(chan, 1)
            for q in QS:
                dve.wait_ge(chan, nth(1, q))
                dve.wait_ge(x_plus, nth(1, q))
                ve.scalar_tensor_tensor(out=XS[q], in0=tile(q, 0), scalar=0.5, in1=XS[q],
                                        op0=ALU.mult, op1=ALU.add).then_inc(x_ready, 1)

            def ffn_block(i, k):
                norm(k, XS, lambda q: (x_ready, nth(2 * i + 1, q)))
                for j in range(HJ):
                    n = HJ * i + j + 1
                    for q in QS:
                        g = tile(q, 2 + j % 2)
                        dve.wait_ge(gate_tanh, nth(n, q))
                        ve.scalar_tensor_tensor(out=g, in0=g, scalar=1.0, in1=PA[q],
                                                op0=ALU.add, op1=ALU.mult).then_inc(gated, 1)
                    for q in QS:
                        dve.wait_ge(gated, nth(n, q))
                        dve.wait_ge(up_out, nth(n, q))
                        ve.tensor_tensor(tile(q, 4 + j), PB[q], tile(q, 2 + j % 2), ALU.mult).then_inc(hidden, 1)
                for q in QS:
                    dve.wait_ge(down_out, nth(i + 1, q))
                    ve.tensor_tensor(XS[q], PA[q], XS[q], ALU.add).then_inc(x_ready, 1)

            ffn_block(0, 3)
            norm(4, XS, lambda q: (x_ready, nth(2, q)), once=[tile(q, 1) for q in QS])
            dve.wait_ge(taps_halved, 1)
            for tap in range(TAPS - 1):
                for q in QS:
                    if tap == 0:
                        dve.wait_ge(conv_begun, nth(1, q))
                    else:
                        dve.wait_ge(conv, nth(tap, q))
                    for h in range(DH):
                        last = ve.scalar_tensor_tensor(out=XC[q][:, h, :], in0=XI[q][:, h, tap:tap + T],
                                                       scalar=v(CONVW + TAPS * h + tap), in1=XC[q][:, h, :],
                                                       op0=ALU.mult, op1=ALU.add)
                    last.then_inc(conv, 1)
                if tap == 0:
                    for q in QS:
                        dve.wait_ge(z_tanh, nth(1, q))
                        ve.scalar_tensor_tensor(out=flat(SZ[q]), in0=flat(SZ[q]), scalar=1.0, in1=flat(PS[q]),
                                                op0=ALU.add, op1=ALU.mult).then_inc(z_silu, 1)
            for q in QS:
                dve.wait_ge(c_tanh, nth(1, q))
                ve.scalar_tensor_tensor(out=flat(XC[q]), in0=flat(tiles(q, 4)), scalar=1.0, in1=flat(XC[q]),
                                        op0=ALU.add, op1=ALU.mult).then_inc(xc_made, 1)
            for q in QS:
                dve.wait_ge(stack1, nth(1, q))
                ve.tensor_tensor(tile(q, 6)[64:P], PA[q][64:P], ST[q][64:P], ALU.subtract).then_inc(rest1, 1)
            for q in QS:
                dve.wait_ge(stack2, nth(1, q))
                ve.tensor_tensor(ST[q][96:P], tile(q, 6)[96:P], ST[q][96:P], ALU.subtract).then_inc(stack3, 1)
            for q in QS:
                dve.wait_ge(dt_exp, nth(1, q))
                dve.wait_ge(stack3, nth(1, q))
                ve.tensor_scalar(tiles(q, 6), tiles(q, 0), 1.0, 1.0, ALU.add, ALU.subtract).then_inc(dt_round, 1)
            for q in QS:
                dve.wait_ge(dt_log1p, nth(1, q))
                ve.scalar_tensor_tensor(out=flat(DT[q]), in0=flat(tiles(q, 2)), scalar=0.0, in1=flat(tiles(q, 4)),
                                        op0=ALU.max, op1=ALU.add).then_inc(dt_made, 1)

            def drive(g, n, r):
                dve.wait_ge(b_spread, n + 1)
                if old(n, RING):
                    dve.wait_ge(scanned, n - RING + 1)
                ve.tensor_tensor(drive_ring[r], DU[g][:], bank_b[:, r % 2, :].unsqueeze(1).to_broadcast([P, DH, T]),
                                 ALU.mult).then_inc(driven, 1)

            def scan(n, r):
                dve.wait_ge(driven, n + 1)
                dve.wait_ge(decayed, n + 1)
                if old(n, RING):
                    dve.wait_ge(weighed, n - RING + 1)
                ve.tensor_tensor_scan(flat(state_ring[r]), flat(decay_ring[r]), flat(drive_ring[r]), 0.0,
                                      ALU.mult, ALU.add).then_inc(scanned, 1)

            def take_y(g):
                dve.wait_ge(y_summed, NS * (g + 1))
                for h in range(DH):
                    last = ve.scalar_tensor_tensor(out=XC[g][:, h, :], in0=XC[g][:, h, :], scalar=v(SKIP + h),
                                                   in1=bank_y[g % 2][:, h, :], op0=ALU.mult, op1=ALU.add)
                last.then_inc(y_taken, 1)

            dve.wait_ge(du_made, B)
            for r in range(RING):
                last = ve.memset(decay_ring[r][:, :, 0:1], 0.0)
            last.then_inc(zeros_set, 1)
            for g in QS:
                for s in range(RING):
                    n = NS * g + s
                    drive(g, n, s)
                    if n >= 1:
                        scan(n - 1, (s - 1) % RING)
                if g >= 1:
                    take_y(g - 1)
                with dve.Fori(1, NS // RING) as i:
                    for r in range(RING):
                        drive(g, NS * g + RING * i + r, r)
                        scan(NS * g + RING * i + r - 1, (r - 1) % RING)
            scan(NS * B - 1, RING - 1)
            take_y(B - 1)
            for q in QS:
                dve.wait_ge(o_out, nth(1, q))
                ve.tensor_tensor(XS[q], PA[q], XS[q], ALU.add).then_inc(x_ready, 1)
            ffn_block(1, 5)

        @block.gpsimd
        def _(pool):
            gp = nc.gpsimd

            def root(k, twice):
                m = 1 + int(twice)
                for q in QS:
                    pool.wait_ge(moments_made, nth(k, q))
                    last = gp.tensor_scalar(rstd[q][:, 0, :], moments[q][:, :, 1], 1.0, EPS, ALU.mult, ALU.add)
                    if twice:
                        last = gp.tensor_scalar(rstd[q][:, 1, :], moments[q][:, :, 1], 1.0 + EPS, EPS * EPS,
                                                ALU.mult, ALU.add)
                    last.then_inc(var_eps, 1)
                    pool.wait_ge(var_eps, nth(k, q))
                    gp.tensor_tensor(rstd[q][:, 0:m, :], rstd[q][:, 0:m, :], power[:, 0:m, :], ALU.pow).then_inc(rstd_made, 1)

            def difference(k):
                for q in QS:
                    pool.wait_ge(h_made, nth(k, q))
                    gp.tensor_tensor(tile(q, 1), H[q][:, 1:T + 1], H[q][:, 0:T], ALU.subtract).then_inc(h_diff, 1)

            pool.wait_ge(power_set, 1)
            root(1, True)
            difference(1)
            for q in QS:
                pool.wait_ge(max_run, nth(1, q))
                gp.tensor_tensor(tile(q, 0), PP[q][:, 0:T], PP[q][:, 1:T + 1], ALU.subtract).then_inc(max_diff, 1)
            for q in QS:
                gp.tensor_tensor(tile(q, 1), tile(q, 5), PP[q][:, 1:T + 1], ALU.subtract).then_inc(max_diff, 1)
            for q in QS:
                pool.wait_ge(wkv_exp, nth(2, q))
                pool.wait_ge(kv_copied, nth(2, q))
                pool.wait_ge(kvr_out, nth(3, q))
                gp.tensor_tensor(tile(q, 4), tile(q, 1), tile(q, 6), ALU.mult).then_inc(v_weighed, 1)
            for q in QS:
                pool.wait_ge(wkv_exp, nth(4, q))
                pool.wait_ge(v_weighed, nth(1, q))
                gp.tensor_tensor(tile(q, 6), tile(q, 2), tile(q, 6), ALU.mult).then_inc(prior, 1)
            for q in QS:
                pool.wait_ge(a_summed, nth(1, q))
                gp.tensor_tensor(tile(q, 1), tile(q, 3), AA[q][:, 2:T + 2], ALU.mult).then_inc(prior, 1)
                pool.wait_ge(prior, nth(2, q))
                gp.tensor_tensor(tile(q, 3), tile(q, 3), BB[q][:, 2:T + 2], ALU.mult).then_inc(num_kept, 1)
                pool.wait_ge(num_kept, nth(1, q))
                gp.tensor_tensor(tile(q, 3), tile(q, 3), tile(q, 2), ALU.add).then_inc(den_made, 1)
            root(2, False)
            for q in QS:
                pool.wait_ge(x_att, nth(1, q))
                gp.tensor_tensor(X[q][:], X[q][:], U[q][:], ALU.add).then_inc(x_plus, 1)
            difference(2)
            root(3, False)
            root(4, True)
            for q in QS:
                pool.wait_ge(normed, nth(4, q))
                gp.tensor_tensor(X[q][:], X[q][:], tile(q, 1), ALU.add).then_inc(x_plus, 1)
            for q in QS:
                pool.wait_ge(dt_round, nth(1, q))
                pool.wait_ge(dt_log, nth(1, q))
                gp.tensor_tensor(tiles(q, 0), tiles(q, 0), tiles(q, 6), ALU.subtract).then_inc(dt_rest, 1)
                pool.wait_ge(dt_rest, nth(1, q))
                gp.tensor_tensor(tiles(q, 4), tiles(q, 4), tiles(q, 0), ALU.add).then_inc(dt_log1p, 1)
            for q in QS:
                pool.wait_ge(dt_made, nth(1, q))
                gp.tensor_tensor(DU[q][:], DT[q][:], XC[q][:], ALU.mult).then_inc(du_made, 1)

            def weigh(n, r):
                pool.wait_ge(scanned, n + 1)
                pool.wait_ge(c_kept, n + 1)
                if old(n, RING):
                    pool.wait_ge(y_summed, n - RING + 1)
                gp.tensor_tensor(term_ring[r], state_ring[r], c_ring[r].unsqueeze(1).to_broadcast([P, DH, T]),
                                 ALU.mult).then_inc(weighed, 1)

            def gate_y(g):
                pool.wait_ge(y_taken, g + 1)
                gp.tensor_tensor(XC[g][:], XC[g][:], SZ[g][:], ALU.mult).then_inc(y_gated, 1)

            pool.wait_ge(z_silu, B)
            for g in QS:
                for s in range(RING):
                    weigh(NS * g + s, s)
                with pool.Fori(1, NS // RING) as i:
                    for r in range(RING):
                        weigh(NS * g + RING * i + r, r)
                if g >= 1:
                    gate_y(g - 1)
            gate_y(B - 1)
            root(5, False)


def kernel(**inputs):
    import ml_dtypes
    import numpy as np
    import concourse.bacc as bacc
    from concourse.bass_utils import run_bass_kernel_spmd

    a = {k: np.asarray(x) for k, x in inputs.items()}

    def A(k):
        return a["L0_attn_a_" + k]

    def M(k):
        return a["L0_attn_b_" + k]

    def halves(w):
        return w.reshape(DH, P, -1).transpose(1, 0, 2)

    vecs = [A(k)[:, None] for k in ("ln1_w", "ln1_b", "ln2_w", "ln2_b", "time_decay", "time_first", "tmk", "tmv", "tmr",
                                    "f_tmk", "f_tmr")]
    vecs += [M("ln_w")[:, None], M("ln_b")[:, None], halves(M("conv_w")).reshape(P, -1)]
    vecs += [halves(M(k)).reshape(P, -1) for k in ("conv_b", "dt_proj_b", "D_skip", "A_log")]
    xp = halves(M("x_proj_w"))
    bc = xp[:, :, RANK:]
    gap = np.zeros((P, DH, 32 - RANK), xp.dtype)
    down = a["L0_ffn_w_down"].T.reshape(HJ, P, C).transpose(1, 0, 2).reshape(P, HID)
    eye = np.eye(P, dtype=np.float32)
    pick = np.zeros((P, 2 * NS, P), ml_dtypes.bfloat16)
    for s in range(2 * NS):
        pick[[32 + s, 64 + s, 96 + s], s, :] = 1
    arrays = {
        "x": A("x").reshape(B * T, C),
        "vec": np.concatenate(vecs, 1),
        "att": np.stack([A(k).T for k in ("att_kw", "att_vw", "att_rw", "att_ow")], 1),
        "fkw": A("f_kw").T,
        "frw": A("f_rw").T,
        "fvw": A("f_vw").T.reshape(RJ, P, C).transpose(1, 0, 2),
        "ffn": np.stack([a["L0_ffn_w_gate"].T, a["L0_ffn_w_up"].T, down], 1),
        "inp": M("in_proj_w"),
        "xpj": np.concatenate([xp[:, :, :RANK], gap, bc, bc, bc], 2),
        "dtw": M("dt_proj_w"),
        "outp": halves(M("out_proj_w")),
        "ident": eye,
        "sel": pick,
    }
    arrays = {f"in_{k}_dram": np.ascontiguousarray(x) for k, x in arrays.items()}
    nc = bacc.Bacc("TRN2", target_bir_lowering=False, num_devices=1)
    args = [nc.dram_tensor(k, x.shape, mybir.dt.from_np(x.dtype), kind="ExternalInput").ap() for k, x in arrays.items()]
    out = nc.dram_tensor("out_dram", (B * T, C), F32, kind="ExternalOutput").ap()
    build(nc, *args, out)
    r = run_bass_kernel_spmd(nc, [arrays], core_ids=[0])
    y = r.results[0]["out_dram"]
    return y.reshape(B, T, C)
```

```python
from contextlib import ExitStack

import concourse.bass as bass
from concourse import mybir

ALU = mybir.AluOpType
ACT = mybir.ActivationFunctionType
F32 = mybir.dt.float32
BF16 = mybir.dt.bfloat16
I32 = mybir.dt.int32

P = 128
B, T, C = 4, 512, 128
NB = T // P
RF = 512
RJ = RF // P
HID = 384
HJ = HID // P
DI = 256
DH = DI // P
RANK, NS, TAPS = 8, 16, 4
RING = 4
LAG = 3
EPS = 1e-5
WSCALE = 1.0 / 127.0

LN1G, LN1B, LN2G, LN2B, DECAY, FIRST, TMK, TMV, TMR, FTMK, FTMR, LNG, LNB = range(13)
CONVW = 13
CONVB = CONVW + DH * TAPS
SKIP = CONVB + DH
ALOG = SKIP + DH
NVEC = ALOG + DH * NS


def nth(k, q):
    return B * (k - 1) + q + 1


def alternate(k, q):
    return nth((k + 1) // 2, q)


def ffn_nth(i, j, q):
    if i == 0:
        return B // 2 * (HJ * (q // 2) + j) + q % 2 + 1
    if q == 0:
        return B * HJ + j + 1
    return B * HJ + HJ + (B - 1) * j + q


def build(nc, x_in, vec_in, att_in, fkw_in, frw_in, fvw_in, ffn_in, inp_in, xpj_in, dtw_in, outp_in,
          ident_in, sel_in, out):
    with ExitStack() as ctx:
        def sb(name, shape, dt=F32):
            return ctx.enter_context(nc.sbuf_tensor(name, shape, dt))

        def sem(name):
            return ctx.enter_context(nc.semaphore(name))

        vec = sb("vec", [P, NVEC])
        att = sb("att", [P, 4, C])
        fkw = sb("fkw", [P, RF])
        frw = sb("frw", [P, C])
        fvw = sb("fvw", [P, RJ, C])
        ffn = sb("ffn", [P, 3, HID])
        ffn_int = sb("ffn_int", [P, 3, HID], I32)
        inp = sb("inp", [P, 2 * DI])
        xpj = sb("xpj", [P, DH, P])
        dtw = sb("dtw", [RANK + 1, DI])
        outp = sb("outp", [P, DH, C])
        eye = sb("eye", [P, P])
        minus_eye = sb("minus_eye", [P, P])
        sel = sb("sel", [P, 2 * NS, P], BF16)
        negw = sb("negw", [P, 1])
        nega = sb("nega", [P, DH * NS])
        power = sb("power", [P, 2, NB])
        rest_mix = sb("rest_mix", [P, 2])
        ident, minus = eye[:, :], minus_eye[:, :]
        other = [ffn[:, 0, j * P:(j + 1) * P] for j in range(2)]
        skip = [fkw[:, h * P:(h + 1) * P] for h in range(DH)]

        QS = range(B)
        stats = [sb(f"stats{q}", [P, NB, 6]) for q in QS]
        moments = [sb(f"moments{q}", [P, NB, 2]) for q in QS]
        rstd = [sb(f"rstd{q}", [P, 2, NB]) for q in QS]
        factor = [sb(f"factor{q}", [P, NB]) for q in QS]
        shift = [sb(f"shift{q}", [P, NB]) for q in QS]
        X = [sb(f"X{q}", [P, T]) for q in QS]
        U = [sb(f"U{q}", [P, T]) for q in QS]
        H = [sb(f"H{q}", [P, T + 1]) for q in QS]
        PP = [sb(f"PP{q}", [P, T + 1]) for q in QS]
        XI = [sb(f"XI{q}", [P, DH, T + 3]) for q in QS]
        XC = [sb(f"XC{q}", [P, DH, T]) for q in QS]
        SZ = [sb(f"SZ{q}", [P, DH, T]) for q in QS]
        DT = [sb(f"DT{q}", [P, DH, T]) for q in QS]
        DU = [sb(f"DU{q}", [P, DH, T]) for q in QS]
        SCR = sb("SCR", [P, 8 * B, T])

        def tile(q, i):
            return SCR[:, 8 * q + i, :]

        def tiles(q, i):
            return SCR[:, 8 * q + i:8 * q + i + 2, :]

        def hn(i, q):
            return XI[q][:, 0, 0:T] if i == 1 else tile(q, 1)

        AA = [XI[q][:, 0, :] for q in QS]
        BB = [XI[q][:, 1, :] for q in QS]
        ST = [H[q][:, 0:T // 2].bitcast(BF16) for q in QS]
        LOW = [U[q][0:RANK + 1, :] for q in QS]

        PS = [ctx.enter_context(nc.psum_tensor(f"PS{q}", [P, 2, T], F32)) for q in QS]
        PA, PB = [PS[q][:, 0, :] for q in QS], [PS[q][:, 1, :] for q in QS]

        decay_ring = [SCR[:, 2 * r:2 * r + 2, :] for r in range(RING)]
        drive_ring = [SCR[:, 2 * (RING + r):2 * (RING + r) + 2, :] for r in range(RING)]
        state_ring = [SCR[:, 2 * (2 * RING + r):2 * (2 * RING + r) + 2, :] for r in range(RING)]
        term_ring = [SCR[:, 2 * (3 * RING + r):2 * (3 * RING + r) + 2, :] for r in range(RING)]
        c_ring = [PP[r][:, 0:T] for r in range(RING)]
        bank_y = [PS[0], PS[1]]
        bank_b, bank_c = PS[2], PS[3]
        bank_o = [PB[0], PB[1], PB[0], PB[3]]

        loaded_v, loaded_m, loaded_a, loaded_f, loaded_q, loaded_s = (
            sem(n) for n in ("loaded_v", "loaded_m", "loaded_a", "loaded_f", "loaded_q", "loaded_s"))
        x_loaded, out_stored = [sem(f"x_loaded{q}") for q in QS], sem("out_stored")
        mean_turned, last_shift = sem("mean_turned"), sem("last_shift")
        minus_set, skip_set, rest_set, split_set = (sem(n) for n in ("minus_set", "skip_set", "rest_set", "split_set"))
        power_set, pads_set, decay_exp, decay_set, a_exp, a_set, dequantised, out_halved, z_halved, taps_halved = (
            sem(n) for n in ("power_set", "pads_set", "decay_exp", "decay_set", "a_exp", "a_set", "dequantised",
                             "out_halved", "z_halved", "taps_halved"))
        stats_made, moments_made, var_eps, rstd_made, normed, turned, x_ready = (
            [sem(f"{n}_even"), sem(f"{n}_odd")]
            for n in ("stats_made", "moments_made", "var_eps", "rstd_made", "normed", "turned", "x_ready"))
        shift_set, plain_made, x_plain, ones_set = (sem(n) for n in ("shift_set", "plain_made", "x_plain", "ones_set"))
        h_made, h_diff, mixed, key_mixed, rec_mixed = (
            sem(n) for n in ("h_made", "h_diff", "mixed", "key_mixed", "rec_mixed"))
        kvr_out, kv_copied, r_tanh, max_run, kept_diff, added_diff, out_diff, out_bound, wkv_exp = (
            sem(n) for n in ("kvr_out", "kv_copied", "r_tanh", "max_run", "kept_diff", "added_diff", "out_diff",
                             "out_bound", "wkv_exp"))
        v_weighed, b_summed, a_summed, num_own, num_kept, den_kept, den_made, den_inv, num_made, num_scaled = (
            sem(n) for n in ("v_weighed", "b_summed", "a_summed", "num_own", "num_kept", "den_kept", "den_made",
                             "den_inv", "num_made", "num_scaled"))
        wkv_made, att_out = sem("wkv_made"), sem("att_out")
        x_att, x_plus, rec_out, rec_tanh, val_out, chan = (
            sem(n) for n in ("x_att", "x_plus", "rec_out", "rec_tanh", "val_out", "chan"))
        keys_out, relu, key_sq = ([sem(f"{n}{m}") for m in range(RJ // 2)] for n in ("keys_out", "relu", "key_sq"))
        hn_made, gate_out, gate_tanh, gated, up_out, hidden, down_out = (
            sem(n) for n in ("hn_made", "gate_out", "gate_tanh", "gated", "up_out", "hidden", "down_out"))
        xn_made, xi_out, conv_begun, z_out, z_kept, z_scaled, z_silu, conv, conv_done, c_tanh, xc_made = (
            sem(n) for n in ("xn_made", "xi_out", "conv_begun", "z_out", "z_kept", "z_scaled", "z_silu", "conv",
                             "conv_done", "c_tanh", "xc_made"))
        xp_out, low_made, stack1, rest1, stack2, stack3, dt_out, dt_in = (
            sem(n) for n in ("xp_out", "low_made", "stack1", "rest1", "stack2", "stack3", "dt_out", "dt_in"))
        dt_exp, dt_log, dt_round, dt_rest, dt_plus, dt_made, du_first, du_made = (
            sem(n) for n in ("dt_exp", "dt_log", "dt_round", "dt_rest", "dt_plus", "dt_made", "du_first",
                             "du_made"))
        zeros_set, b_spread, c_spread, c_kept, decayed, driven, scanned, weighed, y_summed = (
            sem(n) for n in ("zeros_set", "b_spread", "c_spread", "c_kept", "decayed", "driven", "scanned",
                             "weighed", "y_summed"))
        y_gated, o_out = sem("y_gated"), sem("o_out")

        x_view = x_in.rearrange("(q n p) c -> q p n c", q=B, p=P)
        out_view = out.rearrange("(q n p) c -> q p n c", q=B, p=P)

        def blocks(t):
            return t.rearrange("p (n c) -> p n c", c=P)

        def v(col, n=1):
            return vec[:, col:col + n]

        def flat(t):
            return t.rearrange("p a b -> p (a b)")

        def old(n, back):
            return not isinstance(n, int) or n >= back

        block = ctx.enter_context(nc.Block())

        @block.sync
        def _(sp):
            sp.dma_start(blocks(X[0][:, :]), x_view[0]).then_inc(x_loaded[0], 16)
            sp.dma_start(blocks(X[1][:, :]), x_view[1]).then_inc(x_loaded[1], 16)
            sp.dma_start(eye[:], ident_in).then_inc(loaded_m, 16)
            sp.dma_start(att[:], att_in).then_inc(loaded_a, 16)
            sp.dma_start(fkw[:], fkw_in).then_inc(loaded_f, 16)
            sp.dma_start(frw[:], frw_in).then_inc(loaded_f, 16)
            sp.dma_start(fvw[:], fvw_in).then_inc(loaded_f, 16)
            sp.dma_start(inp[:], inp_in).then_inc(loaded_s, 16)
            sp.dma_start(xpj[:], xpj_in).then_inc(loaded_s, 16)
            sp.dma_start(dtw[:], dtw_in).then_inc(loaded_s, 16)
            sp.dma_start(outp[:], outp_in).then_inc(loaded_s, 16)
            sp.dma_start(sel[:], sel_in).then_inc(loaded_s, 16)
            for q in QS:
                sp.wait_ge(x_ready[0], alternate(4, q))
                sp.dma_start(out_view[q], blocks(X[q][:, :])).then_inc(out_stored, 16)
            sp.wait_ge(out_stored, 16 * B)

        @block.tensor
        def _(pe):
            mm = nc.tensor.matmul

            def turn(k, q):
                pe.wait_ge(normed[k % 2], alternate(k, q))
                src = U[q][:, :] if k == 5 else tile(q, 0)
                for n in range(NB):
                    last = nc.tensor.transpose(blocks(PA[q])[:, n, :], blocks(src)[:, n, :], ident)
                last.then_inc(turned[k % 2], 1)

            def add(dst, terms, ready, start=True):
                for j, (w, src) in enumerate(terms):
                    last = mm(dst, w, src, start=(start and j == 0), stop=(j == len(terms) - 1), skip_group_check=True)
                last.then_inc(ready, 1)

            def back(dst, weights, srcs):
                for n in range(NB):
                    for j, (w, src) in enumerate(zip(weights, srcs)):
                        last = mm(blocks(dst)[:, n, :], blocks(src)[:, n, :], w, start=(j == 0),
                                  stop=(j == len(srcs) - 1), skip_group_check=True)
                return last

            pe.wait_ge(loaded_m, 16)
            for q in QS:
                turn(1, q)
            pe.wait_ge(loaded_a, 16)
            for q in QS:
                pe.wait_ge(mixed, nth(1, q))
                mm(PA[q], att[:, 0, :], tile(q, 2), start=True, stop=True).then_inc(kvr_out, 1)
            pe.wait_ge(minus_set, 1)
            for q in QS:
                pe.wait_ge(max_run, nth(1, q))
                add(PA[q], [(minus, PP[q][:, 1:T + 1])], added_diff, start=False)
            pe.wait_ge(split_set, 1)
            for q in QS:
                add(PB[q], [(att[:, 1, :], H[q][:, 1:T + 1]), (other[0], H[q][:, 0:T])], kvr_out)
            for q in QS:
                pe.wait_ge(wkv_exp, nth(2, q))
                add(PA[q], [(att[:, 2, :], H[q][:, 1:T + 1]), (other[1], H[q][:, 0:T])], kvr_out)

            def numerator(q):
                pe.wait_ge(r_tanh, nth(1, q))
                pe.wait_ge(num_own, nth(1, q))
                pe.wait_ge(num_kept, nth(1, q))
                add(PA[q], [(ident, tile(q, 1)), (ident, tile(q, 6))], num_made)

            def att_output(q):
                pe.wait_ge(out_halved, 1)
                pe.wait_ge(wkv_made, nth(1, q))
                pe.wait_ge(kv_copied, nth(2, q))
                pe.wait_ge(plain_made, nth(1, q))
                for n in range(NB):
                    mm(blocks(PB[q])[:, n, :], ident, blocks(U[q])[:, n, :], start=True, stop=False,
                       skip_group_check=True)
                    last = mm(blocks(PB[q])[:, n, :], blocks(tile(q, 6))[:, n, :], att[:, 3, :], start=False, stop=True,
                              skip_group_check=True)
                last.then_inc(att_out, 1)

            def keys(q, j):
                mm(PA[q], fkw[:, j * P:(j + 1) * P], tile(q, 2), start=True, stop=True)
                mm(PB[q], fkw[:, (j + 1) * P:(j + 2) * P], tile(q, 2), start=True, stop=True).then_inc(keys_out[j // 2], 1)

            def first_keys(q):
                pe.wait_ge(loaded_f, 48)
                pe.wait_ge(key_mixed, nth(1, q))
                keys(q, 0)

            def more_keys(q):
                pe.wait_ge(relu[0], nth(1, q))
                keys(q, 2)

            def channel_receptance(q):
                pe.wait_ge(rec_mixed, nth(1, q))
                pe.wait_ge(relu[1], nth(1, q))
                back(PA[q], [frw[:, :]], [tile(q, 3)]).then_inc(rec_out, 1)

            def channel_values(q):
                pe.wait_ge(key_sq[0], nth(1, q))
                pe.wait_ge(key_sq[1], nth(1, q))
                back(PB[q], [fvw[:, j, :] for j in range(RJ)], [tile(q, 4 + j) for j in range(RJ)]).then_inc(val_out, 1)

            def mamba_output(q, n):
                pe.wait_ge(y_gated, q + 1)
                for h in range(DH):
                    last = mm(blocks(bank_o[q])[:, n, :], blocks(XC[q][:, h, :])[:, n, :], outp[:, h, :],
                              start=(h == 0), stop=(h == DH - 1), skip_group_check=True)
                last.then_inc(o_out, 1)

            def gate_up(i, q, j):
                if j == 0:
                    pe.wait_ge(dequantised, 3)
                    pe.wait_ge(hn_made, nth(i + 1, q))
                else:
                    pe.wait_ge(gated, ffn_nth(i, j - 1, q))
                mm(PA[q], ffn[:, 0, j * P:(j + 1) * P], hn(i, q), start=True, stop=True).then_inc(gate_out, 1)
                if j > 0:
                    pe.wait_ge(hidden, ffn_nth(i, j - 1, q))
                elif i == 1 and q == 0:
                    pe.wait_ge(x_ready[1], alternate(3, 2))
                mm(PB[q], ffn[:, 1, j * P:(j + 1) * P], hn(i, q), start=True, stop=True).then_inc(up_out, 1)

            def down(i, q):
                pe.wait_ge(hidden, ffn_nth(i, HJ - 1, q))
                back(PA[q], [ffn[:, 2, j * P:(j + 1) * P] for j in range(HJ)],
                     [tile(q, 4 + j) for j in range(HJ)]).then_inc(down_out, 1)


            def inputs(q):
                pe.wait_ge(loaded_s, 80)
                pe.wait_ge(xn_made, nth(1, q))
                mm(PA[q], inp[:, 0:P], tile(q, 2), start=True, stop=True)
                mm(PB[q], inp[:, P:2 * P], tile(q, 2), start=True, stop=True).then_inc(xi_out, 1)

            def gates(q):
                pe.wait_ge(z_halved, 1)
                pe.wait_ge(conv_begun, nth(1, q))
                mm(PA[q], inp[:, 2 * P:3 * P], tile(q, 2), start=True, stop=True)
                mm(PB[q], inp[:, 3 * P:4 * P], tile(q, 2), start=True, stop=True).then_inc(z_out, 1)

            def x_projection(q):
                pe.wait_ge(z_kept, nth(1, q))
                pe.wait_ge(xc_made, nth(1, q))
                mm(PA[q], xpj[:, 0, :], XC[q][:, 0, :], start=True, stop=False)
                mm(PA[q], xpj[:, 1, :], XC[q][:, 1, :], start=False, stop=True).then_inc(xp_out, 1)

            def dt_projection(q):
                pe.wait_ge(low_made, nth(1, q))
                mm(PB[q], dtw[:, P:DI], LOW[q], start=True, stop=True)
                pe.wait_ge(rest1, nth(1, q))
                mm(PA[q], dtw[:, 0:P], LOW[q], start=True, stop=True).then_inc(dt_out, 1)

            def columns(unit):
                gate_up(0, *unit)

            def turn2(q):
                turn(2, q)

            def turn3(q):
                turn(3, q)

            def first_down(q):
                down(0, q)

            def turn4(q):
                turn(4, q)

            for step, unit in (
                    (numerator, 0), (numerator, 1), (numerator, 2), (att_output, 0), (numerator, 3),
                    (att_output, 1), (turn2, 0), (att_output, 2), (turn2, 1), (first_keys, 0), (more_keys, 0),
                    (first_keys, 1), (channel_receptance, 0), (att_output, 3), (more_keys, 1), (channel_values, 0),
                    (turn2, 2), (channel_receptance, 1), (turn2, 3), (channel_values, 1), (first_keys, 2),
                    (first_keys, 3), (more_keys, 2), (turn3, 0), (more_keys, 3), (channel_receptance, 2),
                    (turn3, 1), (channel_values, 2), (columns, (0, 0)), (channel_receptance, 3),
                    (channel_values, 3), (turn3, 2), (columns, (1, 0)), (columns, (0, 1)), (columns, (1, 1)),
                    (columns, (0, 2)), (columns, (1, 2)), (turn3, 3), (first_down, 0), (first_down, 1),
                    (columns, (2, 0)), (columns, (3, 0)), (columns, (2, 1)), (columns, (3, 1)), (turn4, 0),
                    (columns, (2, 2)), (inputs, 0), (columns, (3, 2)), (first_down, 2), (gates, 0), (turn4, 1),
                    (inputs, 1), (first_down, 3), (turn4, 2), (gates, 1), (x_projection, 0), (inputs, 2),
                    (turn4, 3), (gates, 2), (inputs, 3), (dt_projection, 0), (x_projection, 1), (gates, 3),
                    (dt_projection, 1), (x_projection, 2), (x_projection, 3), (dt_projection, 2),
                    (dt_projection, 3)):
                step(unit)

            def spread(g, n, s, r):
                if old(n, 2):
                    pe.wait_ge(driven, n - 1)
                mm(bank_b[:, r % 2, :], sel[:, s, :], ST[g], start=True, stop=True).then_inc(b_spread, 1)
                if old(n, 2):
                    pe.wait_ge(c_kept, n - 1)
                mm(bank_c[:, r % 2, :], sel[:, NS + s, :], ST[g], start=True, stop=True).then_inc(c_spread, 1)

            def begin_total(g, h):
                mm(bank_y[g % 2][:, h, :], skip[h], XC[g][:, h, :], start=True, stop=False, skip_group_check=True)

            def total(g, n, r, stop=False):
                pe.wait_ge(weighed, n + 1)
                for h in range(DH):
                    last = mm(bank_y[g % 2][:, h, :], ident, term_ring[r][:, h, :], start=False, stop=stop,
                              skip_group_check=True)
                last.then_inc(y_summed, 1)

            pe.wait_ge(stack3, B)
            pe.wait_ge(dt_in, B)
            pe.wait_ge(dt_plus, B)
            pe.wait_ge(skip_set, 1)
            for g in QS:
                for s in range(RING):
                    n = NS * g + s
                    spread(g, n, s, s)
                    if 1 <= s <= DH:
                        if g >= 2:
                            pe.wait_ge(x_ready[1], alternate(3, g - 2))
                        begin_total(g, s - 1)
                    if n >= LAG:
                        total(g if s >= LAG else g - 1, n - LAG, (s - LAG) % RING, stop=(s == LAG - 1))
                with pe.Fori(1, NS // RING - 1) as i:
                    for r in range(RING):
                        spread(g, NS * g + RING * i + r, RING * i + r, r)
                        total(g, NS * g + RING * i + r - LAG, (r - LAG) % RING)
                for s in range(NS - RING, NS):
                    spread(g, NS * g + s, s, s % RING)
                    total(g, NS * g + s - LAG, (s - LAG) % RING)
                    if g >= 1:
                        mamba_output(g - 1, s % RING)

            def last_total(n):
                total(B - 1, n, n % RING, stop=(n == NS * B - 1))

            turn(5, 0)
            last_total(NS * B - 3)
            gate_up(1, 0, 0)
            last_total(NS * B - 2)
            last_total(NS * B - 1)
            gate_up(1, 0, 1)
            for n in range(NB):
                mamba_output(B - 1, n)
            turn(5, 1)
            gate_up(1, 0, 2)
            pe.wait_ge(driven, NS * B)
            turn(5, 2)
            gate_up(1, 1, 0)
            gate_up(1, 2, 0)
            down(1, 0)
            pe.wait_ge(c_kept, NS * B)
            turn(5, 3)
            gate_up(1, 3, 0)
            for j in range(1, HJ):
                for q in QS[1:]:
                    gate_up(1, q, j)
            for q in QS[1:]:
                down(1, q)

        @block.scalar
        def _(act):
            activation = nc.scalar.activation
            act.dma_start(vec[:], vec_in).then_inc(loaded_v, 16)
            act.dma_start(blocks(X[2][:, :]), x_view[2]).then_inc(x_loaded[2], 16)
            act.dma_start(blocks(X[3][:, :]), x_view[3]).then_inc(x_loaded[3], 16)
            act.dma_start(ffn_int[:], ffn_in).then_inc(loaded_q, 16)
            act.wait_ge(loaded_v, 16)
            activation(negw[:], v(DECAY), ACT.Exp).then_inc(decay_exp, 1)
            activation(nega[:], v(ALOG, DH * NS), ACT.Exp).then_inc(a_exp, 1)
            activation(v(CONVW, DH * TAPS + DH), v(CONVW, DH * TAPS + DH), ACT.Copy, scale=0.5).then_inc(taps_halved, 1)

            act.wait_ge(loaded_m, 16)
            activation(minus_eye[:], eye[:], ACT.Copy, scale=-1.0).then_inc(minus_set, 1)
            act.wait_ge(pads_set, 1)
            for q in QS:
                act.wait_ge(turned[1], alternate(1, q))
                activation(H[q][:, 1:T + 1], PA[q], ACT.Identity, bias=v(LN1B), scale=v(LN1G)).then_inc(h_made, 1)
            for q in QS:
                act.wait_ge(kvr_out, nth(1, q))
                activation(tile(q, 5), PA[q], ACT.Copy).then_inc(kv_copied, 1)
            act.wait_ge(decay_set, 1)
            act.wait_ge(loaded_a, 16)
            act.wait_ge(rest_set, 1)
            for j in range(2):
                activation(other[j], att[:, 1 + j, :], ACT.Copy, scale=rest_mix[:, j:j + 1])
                last = activation(att[:, 1 + j, :], att[:, 1 + j, :], ACT.Copy, scale=v(TMV + j))
            last.then_inc(split_set, 1)
            for q in QS:
                act.wait_ge(kept_diff, nth(1, q))
                activation(tile(q, 0), tile(q, 0), ACT.Exp, bias=negw[:, 0:1]).then_inc(wkv_exp, 1)
            for q in QS:
                act.wait_ge(added_diff, nth(1, q))
                activation(tile(q, 1), PA[q], ACT.Exp).then_inc(wkv_exp, 1)
            for q in QS:
                act.wait_ge(kvr_out, nth(2, q))
                activation(tile(q, 6), PB[q], ACT.Copy).then_inc(kv_copied, 1)
            for q in QS:
                act.wait_ge(out_bound, nth(1, q))
                activation(tile(q, 3), tile(q, 3), ACT.Exp).then_inc(wkv_exp, 1)
            for q in QS:
                act.wait_ge(out_bound, nth(2, q))
                activation(tile(q, 2), tile(q, 2), ACT.Exp, scale=-1.0).then_inc(wkv_exp, 1)

            def receptance(q):
                act.wait_ge(kvr_out, nth(3, q))
                activation(tile(q, 7), PA[q], ACT.Tanh, scale=0.5).then_inc(r_tanh, 1)

            def weights(_):
                act.wait_ge(kvr_out, nth(3, B - 1))
                activation(att[:, 3, :], att[:, 3, :], ACT.Copy, scale=0.5).then_inc(out_halved, 1)
                act.wait_ge(loaded_s, 80)
                activation(inp[:, DI:2 * DI], inp[:, DI:2 * DI], ACT.Copy, scale=0.5).then_inc(z_halved, 1)
                act.wait_ge(loaded_q, 16)
                for m in range(3):
                    activation(ffn[:, m, :], ffn_int[:, m, :], ACT.Copy,
                               scale=WSCALE * 0.5 if m == 0 else WSCALE).then_inc(dequantised, 1)

            def first_norm(q):
                act.wait_ge(shift_set, nth(1, q))
                for n in range(NB):
                    last = activation(blocks(U[q])[:, n, :], blocks(X[q])[:, n, :], ACT.Identity,
                                      bias=shift[q][:, n:n + 1], scale=rstd[q][:, 0, n:n + 1])
                last.then_inc(plain_made, 1)

            def take_attention(q):
                act.wait_ge(att_out, nth(1, q))
                activation(U[q][:], PB[q], ACT.Copy).then_inc(x_att, 1)

            def second_h(q):
                act.wait_ge(turned[0], alternate(2, q))
                activation(H[q][:, 1:T + 1], PA[q], ACT.Identity, bias=v(LN2B), scale=v(LN2G)).then_inc(h_made, 1)

            def positive(q, m):
                act.wait_ge(keys_out[m], nth(1, q))
                activation(tiles(q, 4 + 2 * m), PS[q][:], ACT.Relu).then_inc(relu[m], 1)

            def first_positive(q):
                positive(q, 0)

            def second_positive(q):
                positive(q, 1)

            def channel_tanh(q):
                act.wait_ge(rec_out, nth(1, q))
                activation(tile(q, 0), PA[q], ACT.Tanh, scale=0.5).then_inc(rec_tanh, 1)

            def skip_weights(_):
                for h in range(DH):
                    last = activation(skip[h], eye[:], ACT.Copy, scale=v(SKIP + h))
                last.then_inc(skip_set, 1)

            def normed_block(k, q):
                act.wait_ge(turned[k % 2], alternate(k, q))
                activation(hn(k == 5, q), PA[q], ACT.Copy).then_inc(hn_made, 1)

            def gate(i, q, j):
                act.wait_ge(gate_out, ffn_nth(i, j, q))
                if j == 2:
                    act.wait_ge(hidden, ffn_nth(i, 0, q))
                activation(tile(q, 2 + j % 2), PA[q], ACT.Tanh).then_inc(gate_tanh, 1)

            def normed3(q):
                normed_block(3, q)

            def second_norm(q):
                act.wait_ge(turned[0], alternate(4, q))
                activation(tile(q, 2), PA[q], ACT.Identity, bias=v(LNB), scale=v(LNG)).then_inc(xn_made, 1)

            def begin_conv(q):
                act.wait_ge(xi_out, nth(1, q))
                activation(XI[q][:, :, 3:T + 3], PS[q][:], ACT.Copy)
                for h in range(DH):
                    last = activation(XC[q][:, h, :], PS[q][:, h, :], ACT.Identity, bias=v(CONVB + h),
                                      scale=v(CONVW + TAPS * h + TAPS - 1))
                last.then_inc(conv_begun, 1)

            def keep_gate(q):
                act.wait_ge(z_out, nth(1, q))
                activation(SZ[q][:], PS[q][:], ACT.Tanh)
                activation(DT[q][:], PS[q][:], ACT.Copy).then_inc(z_kept, 1)

            def conv_tanh(q):
                act.wait_ge(conv_done, nth(1, q))
                activation(tiles(q, 4), XC[q][:], ACT.Tanh).then_inc(c_tanh, 1)

            def first_part(q):
                act.wait_ge(xp_out, nth(1, q))
                act.wait_ge(ones_set, nth(1, q))
                activation(LOW[q][0:RANK], PA[q][0:RANK], ACT.Copy).then_inc(low_made, 1)
                activation(ST[q], PA[q], ACT.Copy).then_inc(stack1, 1)

            def second_part(q):
                act.wait_ge(rest1, nth(1, q))
                activation(ST[q][64:P], tile(q, 6)[64:P], ACT.Copy).then_inc(stack2, 1)

            def softplus_exp(q):
                act.wait_ge(dt_out, nth(1, q))
                activation(tiles(q, 0), PS[q][:], ACT.Abs).then_inc(dt_in, 1)
                act.wait_ge(dt_in, nth(1, q))
                activation(tiles(q, 0), tiles(q, 0), ACT.Exp, scale=-1.0).then_inc(dt_exp, 1)

            def column_tanh(unit):
                gate(0, *unit)

            for step, unit in (
                    (receptance, 0), (receptance, 1), (receptance, 2), (receptance, 3), (weights, 0),
                    (first_norm, 0), (first_norm, 1), (first_norm, 2), (first_norm, 3), (take_attention, 0),
                    (take_attention, 1), (second_h, 0), (take_attention, 2), (second_h, 1), (first_positive, 0),
                    (second_positive, 0), (first_positive, 1), (channel_tanh, 0), (take_attention, 3),
                    (second_positive, 1), (second_h, 2), (channel_tanh, 1), (second_h, 3), (first_positive, 2),
                    (first_positive, 3), (second_positive, 2), (normed3, 0), (second_positive, 3),
                    (channel_tanh, 2), (normed3, 1), (column_tanh, (0, 0)), (channel_tanh, 3), (skip_weights, 0),
                    (normed3, 2), (column_tanh, (1, 0)), (column_tanh, (0, 1)), (column_tanh, (1, 1)),
                    (column_tanh, (0, 2)), (column_tanh, (1, 2)), (normed3, 3), (column_tanh, (2, 0)),
                    (column_tanh, (3, 0)), (column_tanh, (2, 1)), (column_tanh, (3, 1)), (second_norm, 0),
                    (column_tanh, (2, 2)), (begin_conv, 0), (column_tanh, (3, 2)), (conv_tanh, 0),
                    (second_norm, 1), (keep_gate, 0), (begin_conv, 1), (second_norm, 2), (keep_gate, 1),
                    (first_part, 0), (begin_conv, 2), (conv_tanh, 1), (second_norm, 3), (second_part, 0),
                    (keep_gate, 2), (begin_conv, 3), (conv_tanh, 2), (softplus_exp, 0), (first_part, 1),
                    (keep_gate, 3), (conv_tanh, 3), (second_part, 1), (softplus_exp, 1), (first_part, 2),
                    (first_part, 3), (second_part, 2), (second_part, 3), (softplus_exp, 2), (softplus_exp, 3)):
                step(unit)
            for q in QS:
                act.wait_ge(dt_exp, nth(1, q))
                activation(tiles(q, 4), tiles(q, 0), ACT.Ln, bias=1.0).then_inc(dt_log, 1)

            def unit(g, n, s, r):
                act.wait_ge(c_spread, n + 1)
                if old(n, RING):
                    act.wait_ge(weighed, n - RING + 1)
                activation(c_ring[r], bank_c[:, r % 2, :], ACT.Copy).then_inc(c_kept, 1)
                if old(n, RING):
                    act.wait_ge(scanned, n - RING + 1)
                for h in range(DH):
                    last = activation(decay_ring[r][:, h, 1:T], DT[g][:, h, 1:T], ACT.Exp,
                                      scale=nega[:, bass.ds(NS * h + s, 1)])
                last.then_inc(decayed, 1)

            def residual(q):
                act.wait_ge(normed[0], alternate(4, q))
                for n in range(NB):
                    last = activation(blocks(X[q])[:, n, :], blocks(X[q])[:, n, :], ACT.Identity,
                                      bias=shift[q][:, n:n + 1], scale=factor[q][:, n:n + 1])
                last.then_inc(x_plain, 1)

            def last_norm(q):
                act.wait_ge(last_shift, q + 1)
                act.wait_ge(dt_out, B)
                for n in range(NB):
                    last = activation(blocks(U[q])[:, n, :], blocks(X[q])[:, n, :], ACT.Identity,
                                      bias=shift[q][:, n:n + 1], scale=rstd[q][:, 0, n:n + 1])
                last.then_inc(normed[1], 1)

            act.wait_ge(a_set, 1)
            act.wait_ge(dt_made, 1)
            act.wait_ge(zeros_set, 1)
            for g in QS:
                for s in range(RING):
                    unit(g, NS * g + s, s, s)
                with act.Fori(1, NS // RING) as i:
                    for r in range(RING):
                        unit(g, NS * g + RING * i + r, RING * i + r, r)
                if g >= 2:
                    last_norm(g - 2)
                if g < B - 1:
                    residual(g)
                if g == B - 2:
                    residual(B - 1)
            normed_block(5, 0)
            act.wait_ge(scanned, NS * B)
            gate(1, 0, 0)
            last_norm(B - 2)
            gate(1, 0, 1)
            normed_block(5, 1)
            gate(1, 0, 2)
            normed_block(5, 2)
            act.wait_ge(y_summed, NS * B)
            gate(1, 1, 0)
            last_norm(B - 1)
            gate(1, 2, 0)
            normed_block(5, 3)
            gate(1, 3, 0)
            for j in range(1, HJ):
                for q in QS[1:]:
                    gate(1, q, j)

        @block.vector
        def _(dve):
            ve = nc.vector
            ve.memset(power[:], -0.5).then_inc(power_set, 1)
            for q in QS:
                ve.memset(H[q][:, 0:1], 0.0)
                ve.memset(PP[q][:, 0:1], -1e38)
                last = ve.memset(XI[q][:, :, 0:3], 0.0)
            last.then_inc(pads_set, 1)


            def stats_of(k, src, q):
                for n in range(NB):
                    last = ve.bn_stats(stats[q][:, n, :], blocks(src[q])[:, n, :])
                last.then_inc(stats_made[k % 2], 1)
                dve.wait_ge(stats_made[k % 2], alternate(k, q))
                for n in range(NB):
                    last = ve.bn_aggr(moments[q][:, n, :], stats[q][:, n, :])
                last.then_inc(moments_made[k % 2], 1)

            def normalise(k, src, q, twice=False):
                dve.wait_ge(rstd_made[k % 2], alternate(k, q))
                if twice:
                    ve.tensor_scalar(factor[q][:], rstd[q][:, 0, :], 1.0, None, ALU.add)
                    ve.scalar_tensor_tensor(out=shift[q][:], in0=moments[q][:, :, 0], scalar=-1.0, in1=rstd[q][:, 0, :],
                                            op0=ALU.mult, op1=ALU.mult).then_inc(shift_set, 1)
                for n in range(NB):
                    last = ve.tensor_scalar(blocks(tile(q, 0))[:, n, :], blocks(src[q])[:, n, :], moments[q][:, n, 0:1],
                                            rstd[q][:, int(twice), n:n + 1], ALU.subtract, ALU.mult)
                last.then_inc(normed[k % 2], 1)

            XS, US = [X[q][:, :] for q in QS], [U[q][:, :] for q in QS]

            def first_stats(q):
                dve.wait_ge(x_loaded[q], 16)
                stats_of(1, XS, q)

            for i in range(B + 2):
                if i < B:
                    first_stats(i)
                if i >= 2:
                    normalise(1, XS, i - 2, twice=True)
            dve.wait_ge(loaded_v, 16)
            ve.tensor_scalar(rest_mix[:], v(TMV, 2), -1.0, 1.0, ALU.mult, ALU.add).then_inc(rest_set, 1)
            dve.wait_ge(decay_exp, 1)
            ve.tensor_scalar(negw[:], negw[:], -1.0, None, ALU.mult).then_inc(decay_set, 1)
            dve.wait_ge(a_exp, 1)
            ve.tensor_scalar(nega[:], nega[:], -1.0, None, ALU.mult).then_inc(a_set, 1)

            def mix(q, dst, col, ready):
                ve.scalar_tensor_tensor(out=tile(q, dst), in0=tile(q, 1), scalar=v(col), in1=H[q][:, 0:T],
                                        op0=ALU.mult, op1=ALU.add).then_inc(ready, 1)

            for q in QS:
                dve.wait_ge(h_diff, nth(1, q))
                mix(q, 2, TMK, mixed)
            dve.wait_ge(decay_set, 1)
            for q in QS:
                dve.wait_ge(kv_copied, nth(1, q))
                ve.tensor_tensor_scan(PP[q][:, 1:T + 1], negw[:, 0:1].to_broadcast([P, T]), tile(q, 5),
                                      -1e38, ALU.add, ALU.max).then_inc(max_run, 1)
            for q in QS:
                dve.wait_ge(max_run, nth(1, q))
                ve.scalar_tensor_tensor(out=tile(q, 2), in0=PP[q][:, 0:T], scalar=v(FIRST), in1=tile(q, 5),
                                        op0=ALU.subtract, op1=ALU.subtract).then_inc(out_diff, 1)
            for q in QS:
                dve.wait_ge(out_diff, nth(1, q))
                ve.tensor_scalar(tile(q, 3), tile(q, 2), 0.0, None, ALU.min).then_inc(out_bound, 1)
            for q in QS:
                dve.wait_ge(out_bound, nth(1, q))
                ve.tensor_scalar(tile(q, 2), tile(q, 2), 0.0, None, ALU.max).then_inc(out_bound, 1)
            for q in QS:
                dve.wait_ge(wkv_exp, nth(2, q))
                ve.tensor_tensor_scan(BB[q][:, 3:T + 3], tile(q, 0), tile(q, 1), 0.0,
                                      ALU.mult, ALU.add).then_inc(b_summed, 1)
            for q in QS:
                dve.wait_ge(b_summed, nth(1, q))
                dve.wait_ge(wkv_exp, nth(3, q))
                ve.tensor_tensor(BB[q][:, 2:T + 2], tile(q, 3), BB[q][:, 2:T + 2], ALU.mult).then_inc(den_kept, 1)
            for q in QS:
                dve.wait_ge(v_weighed, nth(1, q))
                ve.tensor_tensor_scan(AA[q][:, 3:T + 3], tile(q, 0), tile(q, 5), 0.0,
                                      ALU.mult, ALU.add).then_inc(a_summed, 1)

            def invert(q):
                dve.wait_ge(den_kept, nth(1, q))
                dve.wait_ge(wkv_exp, nth(4, q))
                dve.wait_ge(a_summed, nth(1, q))
                ve.tensor_tensor(tile(q, 0), BB[q][:, 2:T + 2], tile(q, 2), ALU.add).then_inc(den_made, 1)
                dve.wait_ge(den_made, nth(1, q))
                ve.reciprocal(tile(q, 0), tile(q, 0)).then_inc(den_inv, 1)

            def finish_wkv(q):
                dve.wait_ge(num_made, nth(1, q))
                ve.scalar_tensor_tensor(out=tile(q, 7), in0=tile(q, 7), scalar=1.0, in1=PA[q],
                                        op0=ALU.add, op1=ALU.mult).then_inc(num_scaled, 1)
                dve.wait_ge(den_inv, nth(1, q))
                dve.wait_ge(num_scaled, nth(1, q))
                ve.tensor_tensor(tile(q, 6), tile(q, 7), tile(q, 0), ALU.mult).then_inc(wkv_made, 1)

            def second_stats(q):
                dve.wait_ge(x_att, nth(1, q))
                stats_of(2, US, q)

            def channel_mixes(q):
                dve.wait_ge(h_diff, nth(2, q))
                mix(q, 2, FTMK, key_mixed)
                mix(q, 3, FTMR, rec_mixed)

            def squares(q, m):
                dve.wait_ge(relu[m], nth(1, q))
                ve.tensor_tensor(tiles(q, 4 + 2 * m), tiles(q, 4 + 2 * m), tiles(q, 4 + 2 * m),
                                 ALU.mult).then_inc(key_sq[m], 1)

            def first_squares(q):
                squares(q, 0)

            def second_squares(q):
                squares(q, 1)

            def add_channels(q):
                dve.wait_ge(val_out, nth(1, q))
                dve.wait_ge(rec_tanh, nth(1, q))
                ve.scalar_tensor_tensor(out=tile(q, 0), in0=tile(q, 0), scalar=1.0, in1=PB[q],
                                        op0=ALU.add, op1=ALU.mult).then_inc(chan, 1)
                dve.wait_ge(chan, nth(1, q))
                dve.wait_ge(x_plus, nth(1, q))
                ve.scalar_tensor_tensor(out=XS[q], in0=tile(q, 0), scalar=0.5, in1=XS[q],
                                        op0=ALU.mult, op1=ALU.add).then_inc(x_ready[1], 1)
                dve.wait_ge(x_ready[1], alternate(1, q))
                stats_of(3, XS, q)

            def gated_part(i, q, j):
                g = tile(q, 2 + j % 2)
                dve.wait_ge(gate_tanh, ffn_nth(i, j, q))
                ve.scalar_tensor_tensor(out=g, in0=g, scalar=1.0, in1=PA[q], op0=ALU.add, op1=ALU.mult).then_inc(gated, 1)

            def hidden_part(i, q, j):
                dve.wait_ge(gated, ffn_nth(i, j, q))
                dve.wait_ge(up_out, ffn_nth(i, j, q))
                ve.tensor_tensor(tile(q, 4 + j), PB[q], tile(q, 2 + j % 2), ALU.mult).then_inc(hidden, 1)

            def add_ffn(i, q):
                dve.wait_ge(down_out, nth(i + 1, q))
                ve.tensor_tensor(XS[q], PA[q], XS[q], ALU.add).then_inc(x_ready[0], 1)

            def mamba_stats(q):
                add_ffn(0, q)
                dve.wait_ge(x_ready[0], alternate(2, q))
                stats_of(4, XS, q)

            def convolve(q):
                for tap in range(TAPS - 1):
                    if tap == 0:
                        dve.wait_ge(taps_halved, 1)
                        dve.wait_ge(conv_begun, nth(1, q))
                    else:
                        dve.wait_ge(conv, (TAPS - 2) * q + tap)
                    for h in range(DH):
                        last = ve.scalar_tensor_tensor(out=XC[q][:, h, :], in0=XI[q][:, h, tap:tap + T],
                                                       scalar=v(CONVW + TAPS * h + tap), in1=XC[q][:, h, :],
                                                       op0=ALU.mult, op1=ALU.add)
                    last.then_inc(conv if tap < TAPS - 2 else conv_done, 1)

            def conv_silu(q):
                dve.wait_ge(c_tanh, nth(1, q))
                ve.scalar_tensor_tensor(out=flat(XC[q]), in0=flat(tiles(q, 4)), scalar=1.0, in1=flat(XC[q]),
                                        op0=ALU.add, op1=ALU.mult).then_inc(xc_made, 1)

            def first_rest(q):
                dve.wait_ge(stack1, nth(1, q))
                ve.tensor_tensor(tile(q, 6)[64:P], PA[q][64:P], ST[q][64:P], ALU.subtract).then_inc(rest1, 1)

            def second_rest(q):
                dve.wait_ge(stack2, nth(1, q))
                ve.tensor_tensor(ST[q][96:P], tile(q, 6)[96:P], ST[q][96:P], ALU.subtract).then_inc(stack3, 1)

            def softplus_round(q):
                dve.wait_ge(dt_exp, nth(1, q))
                dve.wait_ge(stack3, nth(1, q))
                ve.tensor_scalar(tiles(q, 6), tiles(q, 0), 1.0, 1.0, ALU.add, ALU.subtract).then_inc(dt_round, 1)

            def softplus_plus(q):
                dve.wait_ge(dt_rest, nth(1, q))
                dve.wait_ge(dt_in, nth(1, q))
                ve.scalar_tensor_tensor(out=tiles(q, 2), in0=PS[q][:], scalar=0.0, in1=tiles(q, 6),
                                        op0=ALU.max, op1=ALU.add).then_inc(dt_plus, 1)

            def column_gated(unit):
                gated_part(0, *unit)

            def column_hidden(unit):
                hidden_part(0, *unit)

            def normalise2(q):
                normalise(2, US, q)

            def normalise3(q):
                normalise(3, XS, q)

            def normalise4(q):
                normalise(4, XS, q, twice=True)

            def softplus(q):
                dve.wait_ge(dt_plus, nth(1, q))
                dve.wait_ge(dt_log, nth(1, q))
                dve.wait_ge(z_silu, nth(1, q))
                ve.tensor_tensor(DT[q][:], tiles(q, 2), tiles(q, 4), ALU.add).then_inc(dt_made, 1)
                if q == 0:
                    dve.wait_ge(dt_made, 1)
                    ve.tensor_tensor(DU[0][:], DT[0][:], XC[0][:], ALU.mult).then_inc(du_first, 1)
                    for r in range(RING):
                        last = ve.memset(decay_ring[r][:, :, 0:1], 0.0)
                    last.then_inc(zeros_set, 1)

            for step, unit in (
                    (invert, 0), (finish_wkv, 0), (invert, 1), (finish_wkv, 1), (second_stats, 0), (invert, 2),
                    (normalise2, 0), (second_stats, 1), (finish_wkv, 2), (normalise2, 1), (channel_mixes, 0),
                    (invert, 3), (channel_mixes, 1), (finish_wkv, 3), (second_squares, 0), (second_stats, 2),
                    (first_squares, 0), (first_squares, 1), (second_stats, 3), (normalise2, 2),
                    (second_squares, 1), (normalise2, 3), (add_channels, 0), (channel_mixes, 2),
                    (channel_mixes, 3), (add_channels, 1), (normalise3, 0), (first_squares, 2), (normalise3, 1),
                    (second_squares, 2), (first_squares, 3), (second_squares, 3), (add_channels, 2),
                    (column_gated, (0, 0)), (column_hidden, (0, 0)), (normalise3, 2), (add_channels, 3),
                    (column_gated, (1, 0)), (column_hidden, (1, 0)), (column_gated, (0, 1)),
                    (column_hidden, (0, 1)), (column_gated, (1, 1)), (column_hidden, (1, 1)), (normalise3, 3),
                    (column_gated, (0, 2)), (column_hidden, (0, 2)), (column_gated, (1, 2)),
                    (column_hidden, (1, 2)), (mamba_stats, 0), (mamba_stats, 1), (column_gated, (2, 0)),
                    (column_hidden, (2, 0)), (column_gated, (3, 0)), (column_hidden, (3, 0)), (normalise4, 0),
                    (column_gated, (2, 1)), (column_hidden, (2, 1)), (column_gated, (3, 1)),
                    (column_hidden, (3, 1)), (normalise4, 1), (column_gated, (2, 2)), (column_hidden, (2, 2)),
                    (convolve, 0), (mamba_stats, 2), (column_gated, (3, 2)), (column_hidden, (3, 2)),
                    (conv_silu, 0), (normalise4, 2), (mamba_stats, 3), (convolve, 1), (normalise4, 3),
                    (first_rest, 0), (convolve, 2), (second_rest, 0), (conv_silu, 1), (convolve, 3),
                    (first_rest, 1), (conv_silu, 2), (softplus_round, 0), (conv_silu, 3), (second_rest, 1),
                    (softplus_round, 1), (first_rest, 2), (first_rest, 3), (second_rest, 2), (softplus_plus, 0),
                    (second_rest, 3), (softplus_round, 2), (softplus_plus, 1), (softplus_round, 3),
                    (softplus_plus, 2), (softplus, 0), (softplus_plus, 3), (softplus, 1), (softplus, 2),
                    (softplus, 3)):
                step(unit)

            def drive(g, n, r):
                dve.wait_ge(b_spread, n + 1)
                if old(n, RING):
                    dve.wait_ge(scanned, n - RING + 1)
                ve.tensor_tensor(drive_ring[r], DU[g][:], bank_b[:, r % 2, :].unsqueeze(1).to_broadcast([P, DH, T]),
                                 ALU.mult).then_inc(driven, 1)

            def scan(n, r):
                dve.wait_ge(driven, n + 1)
                dve.wait_ge(decayed, n + 1)
                if old(n, RING):
                    dve.wait_ge(weighed, n - RING + 1)
                ve.tensor_tensor_scan(flat(state_ring[r]), flat(decay_ring[r]), flat(drive_ring[r]), 0.0,
                                      ALU.mult, ALU.add).then_inc(scanned, 1)

            def gate_y(g):
                dve.wait_ge(y_summed, NS * (g + 1))
                dve.wait_ge(z_silu, nth(1, g))
                if g == 0:
                    dve.wait_ge(du_first, 1)
                ve.tensor_tensor(XC[g][:], bank_y[g % 2][:], SZ[g][:], ALU.mult).then_inc(y_gated, 1)

            def add_mamba(g):
                dve.wait_ge(o_out, NB * (g + 1))
                dve.wait_ge(x_plain, g + 1)
                ve.tensor_tensor(XS[g], bank_o[g], XS[g], ALU.add).then_inc(x_ready[1], 1)
                dve.wait_ge(x_ready[1], alternate(3, g))
                stats_of(5, XS, g)

            dve.wait_ge(dt_made, B)
            dve.wait_ge(du_first, 1)
            for g in QS:
                if g >= 1:
                    dve.wait_ge(du_made, g)
                for s in range(RING):
                    n = NS * g + s
                    drive(g, n, s)
                    if n >= 1:
                        scan(n - 1, (s - 1) % RING)
                if g >= 1:
                    gate_y(g - 1)
                with dve.Fori(1, NS // RING) as i:
                    for r in range(RING):
                        drive(g, NS * g + RING * i + r, r)
                        scan(NS * g + RING * i + r - 1, (r - 1) % RING)
                if g >= 1:
                    add_mamba(g - 1)
            scan(NS * B - 1, RING - 1)
            gated_part(1, 0, 0)
            hidden_part(1, 0, 0)
            gate_y(B - 1)
            gated_part(1, 0, 1)
            hidden_part(1, 0, 1)
            add_mamba(B - 1)
            gated_part(1, 0, 2)
            hidden_part(1, 0, 2)
            for j in range(HJ):
                for q in QS[1:]:
                    gated_part(1, q, j)
                    hidden_part(1, q, j)
                if j == 0:
                    add_ffn(1, 0)
            for q in QS[1:]:
                add_ffn(1, q)

        @block.gpsimd
        def _(pool):
            gp = nc.gpsimd

            def root(k, twice, batches=QS):
                m = 1 + int(twice)
                for q in batches:
                    pool.wait_ge(moments_made[k % 2], alternate(k, q))
                    last = gp.tensor_scalar(rstd[q][:, 0, :], moments[q][:, :, 1], 1.0, EPS, ALU.mult, ALU.add)
                    if twice:
                        last = gp.tensor_scalar(rstd[q][:, 1, :], moments[q][:, :, 1], 1.0 + EPS, EPS * EPS,
                                                ALU.mult, ALU.add)
                    last.then_inc(var_eps[k % 2], 1)
                    pool.wait_ge(var_eps[k % 2], alternate(k, q))
                    gp.tensor_tensor(rstd[q][:, 0:m, :], rstd[q][:, 0:m, :], power[:, 0:m, :], ALU.pow).then_inc(rstd_made[k % 2], 1)

            pool.wait_ge(power_set, 1)
            root(1, True)

            def difference(k, q):
                pool.wait_ge(h_made, nth(k, q))
                gp.tensor_tensor(tile(q, 1), H[q][:, 1:T + 1], H[q][:, 0:T], ALU.subtract).then_inc(h_diff, 1)

            for q in QS:
                difference(1, q)
            for q in QS:
                pool.wait_ge(max_run, nth(1, q))
                gp.tensor_tensor(tile(q, 0), PP[q][:, 0:T], PP[q][:, 1:T + 1], ALU.subtract).then_inc(kept_diff, 1)
            for q in QS:
                pool.wait_ge(wkv_exp, nth(2, q))
                pool.wait_ge(kv_copied, nth(2, q))
                pool.wait_ge(out_diff, nth(1, q))
                gp.tensor_tensor(tile(q, 5), tile(q, 1), tile(q, 6), ALU.mult).then_inc(v_weighed, 1)

            def numerator_parts(q):
                pool.wait_ge(wkv_exp, nth(4, q))
                pool.wait_ge(v_weighed, nth(1, q))
                gp.tensor_tensor(tile(q, 6), tile(q, 2), tile(q, 6), ALU.mult).then_inc(num_own, 1)
                pool.wait_ge(a_summed, nth(1, q))
                gp.tensor_tensor(tile(q, 1), tile(q, 3), AA[q][:, 2:T + 2], ALU.mult).then_inc(num_kept, 1)

            def root2(q):
                root(2, False, [q])

            def second_difference(q):
                difference(2, q)

            def add_streams(q):
                pool.wait_ge(x_att, nth(1, q))
                gp.tensor_tensor(X[q][:], X[q][:], U[q][:], ALU.add).then_inc(x_plus, 1)

            def set_ones(q):
                pool.wait_ge(x_plus, nth(1, q))
                pool.wait_ge(normed[0], alternate(2, q))
                gp.memset(LOW[q], 1.0).then_inc(ones_set, 1)

            def root3(q):
                root(3, False, [q])

            def gate_silu(q):
                pool.wait_ge(z_kept, nth(1, q))
                gp.tensor_tensor(SZ[q][:], SZ[q][:], DT[q][:], ALU.mult).then_inc(z_scaled, 1)
                pool.wait_ge(z_scaled, nth(1, q))
                gp.tensor_tensor(SZ[q][:], SZ[q][:], DT[q][:], ALU.add).then_inc(z_silu, 1)

            def log_rest(q):
                pool.wait_ge(dt_round, nth(1, q))
                gp.tensor_tensor(tiles(q, 6), tiles(q, 0), tiles(q, 6), ALU.subtract).then_inc(dt_rest, 1)

            def root4(q):
                root(4, True, [q])

            for step, unit in (
                    (numerator_parts, 0), (numerator_parts, 1), (numerator_parts, 2), (numerator_parts, 3),
                    (add_streams, 0), (root2, 0), (add_streams, 1), (set_ones, 0), (root2, 1),
                    (second_difference, 0), (set_ones, 1), (add_streams, 2), (second_difference, 1), (root2, 2),
                    (add_streams, 3), (root2, 3), (set_ones, 2), (set_ones, 3), (second_difference, 2),
                    (second_difference, 3), (root3, 0), (root3, 1), (root3, 2), (root3, 3), (root4, 0), (root4, 1),
                    (root4, 2), (gate_silu, 0), (root4, 3), (gate_silu, 1), (gate_silu, 2), (gate_silu, 3),
                    (log_rest, 0), (log_rest, 1), (log_rest, 2), (log_rest, 3)):
                step(unit)
            for q in QS[1:]:
                pool.wait_ge(dt_made, nth(1, q))
                gp.tensor_tensor(DU[q][:], DT[q][:], XC[q][:], ALU.mult).then_inc(du_made, 1)

            def last_root(q):
                root(5, False, [q])
                gp.tensor_scalar(shift[q][:], moments[q][:, :, 0], -1.0, None, ALU.mult).then_inc(mean_turned, 1)
                pool.wait_ge(mean_turned, q + 1)
                pool.wait_ge(rstd_made[1], alternate(5, q))
                gp.tensor_tensor(shift[q][:], shift[q][:], rstd[q][:, 0, :], ALU.mult).then_inc(last_shift, 1)

            def weigh(n, r):
                pool.wait_ge(scanned, n + 1)
                pool.wait_ge(c_kept, n + 1)
                if old(n, RING):
                    pool.wait_ge(y_summed, n - RING + 1)
                gp.tensor_tensor(term_ring[r], state_ring[r], c_ring[r].unsqueeze(1).to_broadcast([P, DH, T]),
                                 ALU.mult).then_inc(weighed, 1)

            for g in QS:
                for s in range(RING):
                    weigh(NS * g + s, s)
                with pool.Fori(1, NS // RING) as i:
                    for r in range(RING):
                        weigh(NS * g + RING * i + r, r)
                if g >= 1:
                    last_root(g - 1)
            last_root(B - 1)


def kernel(**inputs):
    import ml_dtypes
    import numpy as np
    import concourse.bacc as bacc
    from concourse.bass_utils import run_bass_kernel_spmd

    a = {k: np.asarray(x) for k, x in inputs.items()}

    def A(k):
        return a["L0_attn_a_" + k]

    def M(k):
        return a["L0_attn_b_" + k]

    def halves(w):
        return w.reshape(DH, P, -1).transpose(1, 0, 2)

    vecs = [A(k)[:, None] for k in ("ln1_w", "ln1_b", "ln2_w", "ln2_b", "time_decay", "time_first", "tmk", "tmv", "tmr",
                                    "f_tmk", "f_tmr")]
    vecs += [M("ln_w")[:, None], M("ln_b")[:, None], halves(M("conv_w")).reshape(P, -1)]
    vecs += [halves(M(k)).reshape(P, -1) for k in ("conv_b", "D_skip", "A_log")]
    xp = halves(M("x_proj_w"))
    bc = xp[:, :, RANK:]
    gap = np.zeros((P, DH, 32 - RANK), xp.dtype)
    down = a["L0_ffn_w_down"].T.reshape(HJ, P, C).transpose(1, 0, 2).reshape(P, HID)
    eye = np.eye(P, dtype=np.float32)
    pick = np.zeros((P, 2 * NS, P), ml_dtypes.bfloat16)
    for s in range(2 * NS):
        pick[[32 + s, 64 + s, 96 + s], s, :] = 1
    arrays = {
        "x": A("x").reshape(B * T, C),
        "vec": np.concatenate(vecs, 1),
        "att": np.stack([A(k).T for k in ("att_kw", "att_vw", "att_rw", "att_ow")], 1),
        "fkw": A("f_kw").T,
        "frw": A("f_rw").T,
        "fvw": A("f_vw").T.reshape(RJ, P, C).transpose(1, 0, 2),
        "ffn": np.stack([a["L0_ffn_w_gate"].T, a["L0_ffn_w_up"].T, down], 1),
        "inp": M("in_proj_w"),
        "xpj": np.concatenate([xp[:, :, :RANK], gap, bc, bc, bc], 2),
        "dtw": np.concatenate([M("dt_proj_w"), M("dt_proj_b")[None]], 0),
        "outp": halves(M("out_proj_w")),
        "ident": eye,
        "sel": pick,
    }
    arrays = {f"in_{k}_dram": np.ascontiguousarray(x) for k, x in arrays.items()}
    nc = bacc.Bacc("TRN2", target_bir_lowering=False, num_devices=1)
    args = [nc.dram_tensor(k, x.shape, mybir.dt.from_np(x.dtype), kind="ExternalInput").ap() for k, x in arrays.items()]
    out = nc.dram_tensor("out_dram", (B * T, C), F32, kind="ExternalOutput").ap()
    build(nc, *args, out)
    r = run_bass_kernel_spmd(nc, [arrays], core_ids=[0])
    y = r.results[0]["out_dram"]
    return y.reshape(B, T, C)
```
